# Optimizing a Trainium2 kernel written in Bass

```python
import numpy as np
import jax
import jax.numpy as jnp

def _softmax(x, axis=-1):
    return jax.nn.softmax(x, axis=axis)
def _gelu(x):
    return jax.nn.gelu(x, approximate=True)
def _silu(x):
    return jax.nn.silu(x)
def _sigmoid(x):
    return jax.nn.sigmoid(x)
def _layernorm(x, axis=-1, eps=1e-5):
    m = jnp.mean(x, axis=axis, keepdims=True)
    v = jnp.var(x, axis=axis, keepdims=True)
    return (x - m) / jnp.sqrt(v + eps)
def _scatter_add(tgt, idx, src, axis=0):
    return tgt.at[idx].add(src)
def _segment_sum(src, seg, n):
    return jax.ops.segment_sum(src, seg, n)

kernel_name = 'mk_adj_ffn_d1_adj_256_5df999'

def setup_inputs(seed: int = 0):
    np.random.seed(seed)
    _w = jnp.asarray
    def _rec_inputs():
        import jax
        import jax.numpy as jnp
        _gk = jax.random.key(seed)
        x = -0.000929 + 1 * jax.random.normal(jax.random.fold_in(_gk, 1), (8192, 256), jnp.float32)
        _a = jax.random.bernoulli(jax.random.fold_in(_gk, 2), 0.00195312, (8192, 8192))
        _a = jnp.logical_or(_a, jnp.swapaxes(_a, -1, -2))
        _a = jnp.logical_or(_a, jnp.eye(8192, dtype=bool))
        adj = _a.astype(jnp.int32)
        return x, adj
    x, adj = _rec_inputs()
    def _L0_gnn_setup():
        import jax, jax.numpy as jnp
        import numpy as np
        N = 4096
        IN_F = 256
        OUT_F = 64
        HEADS = 4
        NEG_SLOPE = 0.2
        key = jax.random.key(seed)
        k1, k2, k3, k4 = jax.random.split(key, 4)
        x = jax.random.normal(k1, (N, IN_F), dtype=jnp.float32)
        W = jax.random.normal(k2, (HEADS, IN_F, OUT_F), dtype=jnp.float32) * (1.0 / np.sqrt(IN_F))
        a = jax.random.normal(k3, (HEADS, 2 * OUT_F), dtype=jnp.float32) * (1.0 / np.sqrt(2 * OUT_F))
        adj_matrix = jax.random.randint(k4, (N, N), 0, 2, dtype=jnp.int32)
        return {'x': x, 'W': W, 'a': a, 'adj_matrix': adj_matrix}
    _L0_gnn_all = _L0_gnn_setup()
    _L0_gnn_in = {k: v for k, v in _L0_gnn_all.items() if k in ('W', 'a', )}
    del _L0_gnn_all

    def _L0_ffn_setup():
        import jax, jax.numpy as jnp
        import numpy as np
        E = 8
        K = 2
        D = 256
        H = 512
        DOUT = 256
        EPS = 1e-05
        key = jax.random.key(seed)
        ks = jax.random.split(key, 9)
        s = 0.02
        return {'x': jax.random.normal(ks[0], (4, 8192, D), jnp.float32), 'gamma': 1.0 + 0.05 * jax.random.normal(ks[1], (D,), jnp.float32), 'beta': 0.05 * jax.random.normal(ks[2], (D,), jnp.float32), 'Wr': 0.01 * jax.random.normal(ks[3], (D, E), jnp.float32), 'br': jnp.zeros((E,), jnp.float32), 'W1': s * jax.random.normal(ks[4], (E, D, H), jnp.float32), 'b1': s * jax.random.normal(ks[5], (E, H), jnp.float32), 'W2': s * jax.random.normal(ks[6], (E, H, DOUT), jnp.float32), 'b2': s * jax.random.normal(ks[7], (E, DOUT), jnp.float32)}
    _L0_ffn_all = _L0_ffn_setup()
    _L0_ffn_in = {k: v for k, v in _L0_ffn_all.items() if k in ('gamma', 'beta', 'Wr', 'br', 'W1', 'b1', 'W2', 'b2', )}
    del _L0_ffn_all

    return {
        "x": x,
        "adj": adj,
        "L0_gnn_W": _L0_gnn_in["W"],
        "L0_gnn_a": _L0_gnn_in["a"],
        "L0_ffn_gamma": _L0_ffn_in["gamma"],
        "L0_ffn_beta": _L0_ffn_in["beta"],
        "L0_ffn_Wr": _L0_ffn_in["Wr"],
        "L0_ffn_br": _L0_ffn_in["br"],
        "L0_ffn_W1": _L0_ffn_in["W1"],
        "L0_ffn_b1": _L0_ffn_in["b1"],
        "L0_ffn_W2": _L0_ffn_in["W2"],
        "L0_ffn_b2": _L0_ffn_in["b2"],
    }

def reference(x, adj, L0_gnn_W, L0_gnn_a, L0_ffn_gamma, L0_ffn_beta, L0_ffn_Wr, L0_ffn_br, L0_ffn_W1, L0_ffn_b1, L0_ffn_W2, L0_ffn_b2):
    import jax
    import jax.numpy as jnp
    def _L0_gnn_ref(x, W, a, adj_matrix):
        import jax, jax.numpy as jnp
        import numpy as np
        N = 4096
        IN_F = 256
        OUT_F = 64
        HEADS = 4
        NEG_SLOPE = 0.2
        heads, in_f, out_f = W.shape
        n = x.shape[0]
        xt = jnp.einsum('ni,hio->hno', x, W)
        src = jnp.einsum('hnf,hf->hn', xt, a[:, :out_f])
        dst = jnp.einsum('hnf,hf->hn', xt, a[:, out_f:])
        e = jax.nn.leaky_relu(src[:, :, None] + dst[:, None, :], NEG_SLOPE)
        mask = (adj_matrix > 0)[None, :, :]
        e = jnp.where(mask, e, -jnp.inf)
        attention = jax.nn.softmax(e, axis=2)
        h_prime = jnp.einsum('hij,hjf->hif', attention, xt)
        return h_prime.transpose(1, 0, 2).reshape(n, heads * out_f)

    def _L0_ffn_ref(x, gamma, beta, Wr, br, W1, b1, W2, b2):
        import jax, jax.numpy as jnp
        import numpy as np
        E = 8
        K = 2
        D = 256
        H = 512
        DOUT = 256
        EPS = 1e-05
        mu = jnp.mean(x, axis=-1, keepdims=True)
        var = jnp.mean(jnp.square(x - mu), axis=-1, keepdims=True)
        xn = (x - mu) * jax.lax.rsqrt(var + EPS) * gamma + beta
        logits = jnp.einsum('bsd,de->bse', xn, Wr) + br
        top_vals, top_idx = jax.lax.top_k(logits, K)
        w = jax.nn.softmax(top_vals, axis=-1)
        w_full = jnp.einsum('bsk,bske->bse', w, jax.nn.one_hot(top_idx, E, dtype=w.dtype))
        y = jnp.zeros(x.shape[:-1] + (DOUT,), x.dtype)
        for e in range(E):
            h = jax.nn.gelu(jnp.einsum('bsd,dh->bsh', xn, W1[e]) + b1[e], approximate=False)
            y_e = jnp.einsum('bsh,hd->bsd', h, W2[e]) + b2[e]
            y = y + y_e * w_full[..., e, None]
        return y

    x = x + _L0_gnn_ref(_layernorm(x, axis=-1), L0_gnn_W, L0_gnn_a, adj)
    x = x + _L0_ffn_ref((_layernorm(x, axis=-1))[None], L0_ffn_gamma, L0_ffn_beta, L0_ffn_Wr, L0_ffn_br, L0_ffn_W1, L0_ffn_b1, L0_ffn_W2, L0_ffn_b2)[0]
    return x


_drawn_inputs = setup_inputs


def setup_inputs(seed=0):
    import zlib

    import numpy as np

    out = dict(_drawn_inputs(seed))
    spreads = {'L0_ffn_br': (0.0, 0.1)}
    factors = {'L0_ffn_gamma': 5.943, 'L0_ffn_beta': 5.066, 'L0_ffn_b1': 8.0, 'L0_ffn_b2': 4.321}
    for name, (base, spread) in spreads.items():
        noise = np.random.default_rng([zlib.crc32(name.encode()), seed]).standard_normal(out[name].shape)
        drawn = base * np.exp(spread * noise) if base else spread * noise
        out[name] = jnp.asarray(drawn.astype(out[name].dtype))
    for name, factor in factors.items():
        out[name] = (out[name] * factor).astype(out[name].dtype)
    return out
```

```python
from contextlib import ExitStack

import concourse.bass as bass
from concourse import mybir

F32 = mybir.dt.float32
F32R = mybir.dt.float32r
BF16 = mybir.dt.bfloat16
F16 = mybir.dt.float16
U32 = mybir.dt.uint32
ALU = mybir.AluOpType
ACT = mybir.ActivationFunctionType
AX = mybir.AxisListType.X
ABSMAX = bass.bass_isa.ReduceOp.absmax
RMAX = bass.bass_isa.ReduceOp.max

P = 128
SLOPE = 0.2
LN_EPS = 1e-5
SHARP = 2.0 ** 60
HALF_TOP = 2.0 ** 14

TILES = 4
CH = TILES * P


def make_identity(nc, pool, ident, written):
    nc.gpsimd.memset(ident[:, :], 0.0).then_inc(written, 1)
    pool.wait_ge(written, 1)
    nc.gpsimd.affine_select(out=ident[:, :], in_=ident[:, :], compare_op=ALU.not_equal, fill=1.0,
                            base=0, pattern=[[-1, P]], channel_multiplier=1).then_inc(written, 1)


def turns(eng, chunks, chunk):
    for slot in range(2):
        chunk(0, slot)
    with eng.Fori(1, chunks // 2) as i:
        for slot in range(2):
            chunk(i, slot)


def project(nc, x, gnn_w, gnn_a, xt_dram, s_dram, keep):
    N, D = x.shape
    H, _, O = gnn_w.shape
    NT, NC, KD = N // P, N // CH, D // P
    W1 = H * O + 2 * H
    cE, cF, dsharp, E, F = keep["cE"], keep["cF"], keep["dsharp"], keep["E"], keep["F"]
    with ExitStack() as ctx:
        def sb(name, shape, dt=F32):
            return ctx.enter_context(nc.sbuf_tensor(name, shape, dt))

        def ps(name, shape, dt=F32):
            return ctx.enter_context(nc.psum_tensor(name, shape, dt))

        def sem(name):
            return ctx.enter_context(nc.semaphore(name))

        ident = sb("p_ident", [P, P])
        wext = sb("p_wext", [P, KD, W1])
        wprod = sb("p_wprod", [P, H, 2, O])
        arow = sb("p_arow", [P, H, 2, O])
        eps = sb("p_eps", [P, 1])
        xin = [sb(f"p_xin{k}", [P, TILES, D]) for k in range(2)]
        xn = [sb(f"p_xn{k}", [P, TILES, D]) for k in range(2)]
        stats = [sb(f"p_stats{k}", [P, TILES, 6]) for k in range(2)]
        meanvar = [sb(f"p_meanvar{k}", [P, TILES, 2]) for k in range(2)]
        std = [sb(f"p_std{k}", [P, TILES]) for k in range(2)]
        rstd = [sb(f"p_rstd{k}", [P, TILES]) for k in range(2)]
        xnT = [sb(f"p_xnT{k}", [P, KD, CH]) for k in range(2)]
        xto = [sb(f"p_xto{k}", [P, TILES, W1]) for k in range(2)]
        srcdst = sb("p_srcdst", [P, NT, 2 * H])
        vpart = sb("p_vpart", [P, NC])
        top = sb("p_top", [P, H + 1])
        gtop = sb("p_gtop", [P, H + 1])
        vclip = sb("p_vclip", [P, 1])
        vinv = sb("p_vinv", [P, 1])
        alpha = sb("p_alpha", [P, 1])
        dE = sb("p_dE", [P, NT, H])
        z = sb("p_z", [P, NT, H])
        z5 = sb("p_z5", [P, NT, H])
        m = sb("p_m", [P, NT, H])
        srow = sb("p_srow", [NT, H, P])
        psX = ps("p_psX", [P, KD, CH])
        psP = ps("p_psP", [P, TILES, 512])
        psS = ps("p_psS", [P, H, P])

        s_w = sem("p_w_loaded")
        s_a = sem("p_a_loaded")
        s_id = sem("p_identity")
        s_const = sem("p_const")
        s_fold = sem("p_fold")
        s_carry = sem("p_wait_carrier")
        s_x = [sem("p_x_loaded0"), sem("p_x_loaded1")]
        s_stats = sem("p_stats_ready")
        s_aggr = sem("p_aggr_ready")
        s_std = sem("p_std_ready")
        s_rstd = sem("p_rstd_ready")
        s_xn = sem("p_xn_ready")
        s_xps = sem("p_xT_in_psum")
        s_xT = sem("p_xT_ready")
        s_pp = sem("p_proj_in_psum")
        s_xto = sem("p_xt_ready")
        s_sd = sem("p_srcdst_ready")
        s_xtst = [sem("p_xt_stored0"), sem("p_xt_stored1")]
        s_vp = sem("p_vpart_ready")
        s_top = sem("p_top_ready")
        s_gtop = sem("p_gtop_ready")
        s_f = sem("p_factor_steps")
        s_act = sem("p_factor_exps")
        s_st = sem("p_srcT_in_psum")
        s_srow = sem("p_srow_ready")
        s_sst = sem("p_src_stored")

        xt_v = xt_dram.rearrange("(c t p) f -> c p t f", p=P, t=TILES)
        x_v = x.rearrange("(c t p) d -> c p t d", p=P, t=TILES)
        block = ctx.enter_context(nc.Block())

        @block.gpsimd
        def _(pool):
            make_identity(nc, pool, ident, s_id)
            nc.gpsimd.memset(eps[:, :], LN_EPS).then_inc(s_const, 1)
            pool.wait_ge(s_top, H + 1)
            nc.gpsimd.partition_all_reduce(gtop[:, :], top[:, :], P, RMAX).then_inc(s_gtop, 1)

        @block.sync
        def _(sp):
            for k in range(KD):
                sp.dma_start(wext[:, k, 0:H * O].rearrange("p (h o) -> p h o", h=H),
                             gnn_w[:, k * P:(k + 1) * P, :].rearrange("h p o -> p h o")).then_inc(s_w, 16)
            sp.dma_start(arow[:, :, :, :].rearrange("p h s o -> p (h s o)"),
                         gnn_a.rearrange("(u h) f -> u (h f)", u=1).broadcast_to([P, H * 2 * O])
                         ).then_inc(s_a, 16)
            for c in range(2):
                sp.dma_start(xin[c][:, :, :], x_v[c]).then_inc(s_x[c], 16)
            with sp.Fori(0, NC // 2 - 1) as i:
                for slot in range(2):
                    c = 2 * i + slot
                    sp.wait_ge(s_xn, c + 1)
                    sp.dma_start(xin[slot][:, :, :], x_v[c + 2]).then_inc(s_x[slot], 16)
            sp.wait_ge(s_srow, 1)
            sp.dma_start(s_dram.rearrange("h (t p) -> t h p", p=P), srow[:, :, :]).then_inc(s_sst, 16)
            sp.wait_ge(s_sst, 16)

        @block.vector
        def _(dve):
            dve.wait_ge(s_w, 16 * KD)
            dve.wait_ge(s_a, 16)
            for k in range(KD):
                w3 = wext[:, k, 0:H * O].rearrange("p (h o) -> p h o", h=H)
                if k:
                    dve.wait_ge(s_fold, 3 * k)
                for half in range(2):
                    nc.vector.tensor_tensor(wprod[:, :, half, :], w3, arow[:, :, half, :],
                                            ALU.mult).then_inc(s_fold, 1)
                dve.wait_ge(s_fold, 3 * k + 2)
                nc.vector.tensor_reduce(wext[:, k, H * O:W1].rearrange("p (s h) -> p h s", s=2),
                                        wprod[:, :, :, :], AX, ALU.add).then_inc(s_fold, 1)
            def chunk(i, slot):
                c = 2 * i + slot
                dve.wait_ge(s_x[slot], 16 * i + 16)
                for t in range(TILES):
                    last = nc.vector.bn_stats(stats[slot][:, t, :], xin[slot][:, t, :])
                last.then_inc(s_stats, 1)
                dve.wait_ge(s_stats, c + 1)
                dve.sem_inc(s_carry, 1)
                for t in range(TILES):
                    last = nc.vector.bn_aggr(meanvar[slot][:, t, :], stats[slot][:, t, :])
                last.then_inc(s_aggr, 1)
                dve.wait_ge(s_std, c + 1)
                nc.vector.reciprocal(rstd[slot][:, :], std[slot][:, :]).then_inc(s_rstd, 1)
                dve.wait_ge(s_rstd, c + 1)
                for t in range(TILES):
                    last = nc.vector.tensor_scalar(xn[slot][:, t, :], xin[slot][:, t, :],
                                                   meanvar[slot][:, t, 0:1], rstd[slot][:, t:t + 1],
                                                   ALU.subtract, ALU.mult)
                last.then_inc(s_xn, 1)
                dve.wait_ge(s_xto, c + 1)
                nc.vector.tensor_reduce(vpart[:, bass.ds(c, 1)], xto[slot][:, :, 0:H * O], mybir.AxisListType.XY,
                                        ALU.max, apply_absolute_value=True).then_inc(s_vp, 1)
                nc.vector.tensor_copy(srcdst[:, bass.ds(c * TILES, TILES), :],
                                      xto[slot][:, :, H * O:W1]).then_inc(s_sd, 1)

            turns(dve, NC, chunk)
            dve.wait_ge(s_sd, NC)
            dve.wait_ge(s_vp, NC)
            src = srcdst[:, :, 0:H]
            dst = srcdst[:, :, H:2 * H]
            for h in range(H):
                nc.vector.tensor_reduce(top[:, h:h + 1], srcdst[:, :, H + h], AX, ALU.max).then_inc(s_top, 1)
            nc.vector.tensor_reduce(top[:, H:H + 1], vpart[:, :], AX, ALU.max).then_inc(s_top, 1)
            dve.wait_ge(s_st, 1)
            nc.vector.tensor_copy(srow[:, :, :], psS[0:NT, :, :]).then_inc(s_srow, 1)
            dve.wait_ge(s_gtop, 1)
            D_b = gtop[:, 0:H].unsqueeze(1).broadcast_to([P, NT, H])
            nc.vector.tensor_tensor(dE[:, :, :], dst, D_b, ALU.subtract).then_inc(s_f, 1)
            nc.vector.tensor_tensor(z[:, :, :], src, D_b, ALU.add).then_inc(s_f, 1)
            nc.vector.tensor_scalar(vclip[:, :], gtop[:, H:H + 1], 1.0, None, ALU.max).then_inc(s_f, 1)
            nc.vector.tensor_scalar(dsharp[:, :, :], dst, SHARP, None, ALU.mult).then_inc(s_f, 1)
            dve.wait_ge(s_f, 4)
            nc.vector.reciprocal(vinv[:, :], vclip[:, :]).then_inc(s_f, 1)
            nc.vector.tensor_scalar(z5[:, :, :], z[:, :, :], SLOPE, None, ALU.mult).then_inc(s_f, 1)
            dve.wait_ge(s_f, 6)
            nc.vector.tensor_scalar(alpha[:, :], vinv[:, :], HALF_TOP, None, ALU.mult).then_inc(s_f, 1)
            nc.vector.tensor_tensor(m[:, :, :], z[:, :, :], z5[:, :, :], ALU.max).then_inc(s_f, 1)
            dve.wait_ge(s_f, 8)
            nc.vector.tensor_tensor(z[:, :, :], z[:, :, :], m[:, :, :], ALU.subtract).then_inc(s_f, 1)
            nc.vector.tensor_tensor(z5[:, :, :], z5[:, :, :], m[:, :, :], ALU.subtract).then_inc(s_f, 1)
            dve.wait_ge(s_act, 2)
            nc.vector.tensor_scalar(E[:, :, :], E[:, :, :], alpha[:, 0:1], None, ALU.mult).then_inc(s_f, 1)
            nc.vector.tensor_scalar(F[:, :, :], F[:, :, :], alpha[:, 0:1], None, ALU.mult).then_inc(s_f, 1)

        @block.scalar
        def _(act):
            act.wait_ge(s_const, 1)
            def chunk(i, slot):
                c = 2 * i + slot
                later = not isinstance(c, int) or c > 0
                turn_later = not isinstance(i, int)
                act.wait_ge(s_aggr, c + 1)
                nc.scalar.activation(std[slot][:, :], meanvar[slot][:, :, 1], ACT.Sqrt,
                                     bias=eps[:, 0:1]).then_inc(s_std, 1)
                act.wait_ge(s_xps, c + 1)
                nc.scalar.activation(xnT[slot][:, :, :], psX[:, :, :], ACT.Copy).then_inc(s_xT, 1)
                act.wait_ge(s_pp, c + 1)
                if turn_later:
                    act.wait_ge(s_xtst[slot], 16 * i)
                if later:
                    act.wait_ge(s_sd, c)
                nc.scalar.activation(xto[slot][:, :, :], psP[:, :, 0:W1], ACT.Copy).then_inc(s_xto, 1)
                act.wait_ge(s_xto, c + 1)
                act.dma_start(xt_v[c], xto[slot][:, :, 0:H * O]).then_inc(s_xtst[slot], 16)

            turns(act, NC, chunk)
            act.wait_ge(s_f, 1)
            nc.scalar.activation(E[:, :, :], dE[:, :, :], ACT.Exp).then_inc(s_act, 1)
            nc.scalar.activation(F[:, :, :], dE[:, :, :], ACT.Exp, scale=SLOPE).then_inc(s_act, 1)
            act.wait_ge(s_f, 10)
            nc.scalar.activation(cE[:, :, :], z[:, :, :], ACT.Exp).then_inc(s_act, 1)
            nc.scalar.activation(cF[:, :, :], z5[:, :, :], ACT.Exp).then_inc(s_act, 1)
            for slot in range(2):
                act.wait_ge(s_xtst[slot], 16 * (NC // 2))

        @block.tensor
        def _(pe):
            pe.wait_ge(s_id, 2)
            pe.wait_ge(s_fold, 3 * KD)
            def chunk(i, slot):
                c = 2 * i + slot
                later = not isinstance(c, int) or c > 0
                pe.wait_ge(s_xn, c + 1)
                if later:
                    pe.wait_ge(s_xT, c)
                for t in range(TILES):
                    for k in range(KD):
                        last = nc.tensor.transpose(psX[:, k, t * P:(t + 1) * P],
                                                   xn[slot][:, t, k * P:(k + 1) * P], ident[:, :])
                last.then_inc(s_xps, 1)
                pe.wait_ge(s_xT, c + 1)
                if later:
                    pe.wait_ge(s_xto, c)
                for t in range(TILES):
                    for k in range(KD):
                        last = nc.tensor.matmul(psP[:, t, 0:W1], xnT[slot][:, k, t * P:(t + 1) * P],
                                                wext[:, k, :], start=(k == 0), stop=(k == KD - 1))
                last.then_inc(s_pp, 1)

            turns(pe, NC, chunk)
            pe.wait_ge(s_sd, NC)
            for h in range(H):
                last = nc.tensor.transpose(psS[0:NT, h, :], srcdst[:, :, h], ident[:, :])
            last.then_inc(s_st, 1)


def split_rows(nc, xt_dram, V, keep, N, H, O):
    NT, NC = N // P, N // CH
    E, F = keep["E"], keep["F"]
    with ExitStack() as ctx:
        def sb(name, shape, dt=F32):
            return ctx.enter_context(nc.sbuf_tensor(name, shape, dt))

        def sem(name):
            return ctx.enter_context(nc.semaphore(name))

        xt = [sb(f"v_xt{k}", [P, TILES, H, O]) for k in range(2)]
        prod = [sb(f"v_prod{k}", [P, TILES, H, O]) for k in range(2)]
        s_xt = [sem("v_xt_loaded0"), sem("v_xt_loaded1")]
        s_prod = sem("v_prod_ready")
        s_hi = sem("v_hi_ready")
        s_lo = sem("v_lo_ready")
        s_one = sem("v_ones_hi")
        s_onelo = sem("v_ones_lo")
        xt_v = xt_dram.rearrange("(c t p) f -> c p t f", p=P, t=TILES)
        block = ctx.enter_context(nc.Block())

        @block.sync
        def _(sp):
            def load(c, slot):
                sp.dma_start(xt[slot][:, :, :, :].rearrange("p t h o -> p t (h o)"),
                             xt_v[c]).then_inc(s_xt[slot], 16)

            load(0, 0)
            load(1, 1)
            with sp.Fori(0, NC // 2 - 1) as i:
                for slot in range(2):
                    sp.wait_ge(s_prod, 2 * (2 * i + slot) + 2)
                    load(2 * i + slot + 2, slot)

        @block.scalar
        def _(act):
            for k, fac in enumerate((E, F)):
                last = nc.scalar.activation(V[:, :, 2 * k, :, O], fac[:, :, :], ACT.Copy)
            last.then_inc(s_one, 1)
            with act.Fori(0, NC // 2) as i:
                for slot in range(2):
                    c = 2 * i + slot
                    for k in range(2):
                        act.wait_ge(s_prod, 2 * c + k + 1)
                        for t in range(TILES):
                            last = nc.scalar.activation(V[:, bass.ds(c * TILES + t, 1), 2 * k, :, 0:O],
                                                        prod[k][:, t:t + 1, :, :], ACT.Copy)
                        last.then_inc(s_hi, 1)

        @block.vector
        def _(dve):
            dve.wait_ge(s_one, 1)
            for k, fac in enumerate((E, F)):
                nc.vector.tensor_tensor(V[:, :, 2 * k + 1, :, O], fac[:, :, :], V[:, :, 2 * k, :, O],
                                        ALU.subtract).then_inc(s_onelo, 1)

            def chunk(i, slot, first):
                c = 2 * i + slot
                dve.wait_ge(s_xt[slot], 16 * i + 16)
                for k, fac in enumerate((E, F)):
                    if not first:
                        dve.wait_ge(s_lo, 2 * c + k - 1)
                    fb = fac[:, bass.ds(c * TILES, TILES), :].unsqueeze(3).broadcast_to([P, TILES, H, O])
                    nc.vector.tensor_tensor(prod[k][:, :, :, :], xt[slot][:, :, :, :], fb,
                                            ALU.mult).then_inc(s_prod, 1)
                for k in range(2):
                    dve.wait_ge(s_hi, 2 * c + k + 1)
                    jb = bass.ds(c * TILES, TILES)
                    nc.vector.tensor_tensor(V[:, jb, 2 * k + 1, :, 0:O], prod[k][:, :, :, :],
                                            V[:, jb, 2 * k, :, 0:O], ALU.subtract).then_inc(s_lo, 1)

            chunk(0, 0, True)
            chunk(0, 1, False)
            with dve.Fori(1, NC // 2) as i:
                for slot in range(2):
                    chunk(i, slot, False)


def attend(nc, x, adj, s_dram, x1_dram, V, keep, H, O):
    N, D = x.shape
    NT, NC = N // P, N // CH
    PAIRS = NT // 2
    COLS = 4 * P
    LOADS = N // COLS
    PPL = COLS // P // 2
    O1 = O + 1
    EXPLICIT = 3
    IMPLICIT = H - EXPLICIT
    TH = TILES * H
    PER = 512 // O1
    NG = 2 * TH + TILES * IMPLICIT
    NB = -(-NG // PER)
    NBA = NB // 2
    STEPS = 6
    cE, cF, dsharp = keep["cE"], keep["cF"], keep["dsharp"]
    with ExitStack() as ctx:
        def sb(name, shape, dt=F32):
            return ctx.enter_context(nc.sbuf_tensor(name, shape, dt))

        def sem(name):
            return ctx.enter_context(nc.semaphore(name))

        ident = sb("g_ident", [P, P], BF16)
        araw = [sb(f"g_araw{k}", [P, TILES, COLS], BF16) for k in range(2)]
        src_head = sb("g_src_head", [P, H, CH])
        src_rest = sb("g_src_rest", [P, H, CH])
        step = [sb(f"g_step{k}", [P, 2, CH], F16) for k in range(2)]
        A = [sb(f"g_A{k}", [P, 2, CH], F16) for k in range(2)]
        B = [[sb(f"g_B{k}_{h}", [P, 2, CH], F16) for h in range(H)] for k in range(2)]
        C = [[sb(f"g_C{k}_{h}", [P, 2, CH], F16) for h in range(EXPLICIT)] for k in range(2)]
        sums = sb("g_sums", [P, NG, O1])
        den = sb("g_den", [P, 2, TH])
        rden = sb("g_rden", [P, TH])
        xrow = sb("g_xrow", [P, TH, O])
        acc = ctx.enter_context(nc.psum_tensor("g_acc", [P, NB, 512], F32))
        turned = [ctx.enter_context(nc.psum_tensor(f"g_turned{k}", [P, 2, CH], BF16)) for k in range(2)]

        s_id = sem("g_identity")
        s_adj = [sem("g_adj_loaded0"), sem("g_adj_loaded1")]
        s_head = sem("g_src_head_loaded")
        s_rest = sem("g_src_rest_loaded")
        s_turn = sem("g_turned_pairs")
        s_A = sem("g_A_ready")
        s_step = sem("g_step_ready")
        s_B = sem("g_B_ready")
        s_masks = sem("g_masks_ready")
        s_used = sem("g_masks_used")
        s_sumA = sem("g_sums_by_act")
        s_sumD = sem("g_sums_by_dve")
        s_den = sem("g_den_steps")
        s_post = sem("g_post_steps")
        s_x = sem("g_x_loaded")
        s_out = sem("g_x1_stored")
        s_carry = sem("g_wait_carrier")

        adj_v = adj.rearrange("(c t p) (l j) -> c l p t j", p=P, t=TILES, j=COLS)
        x_v = x.rearrange("(c t p) d -> c p t d", p=P, t=TILES)
        x1_v = x1_dram.rearrange("(c t p) d -> c p t d", p=P, t=TILES)
        xrow_v = xrow[:, :, :].rearrange("p (t h) o -> p t (h o)", t=TILES)

        def slot_of(g):
            return acc[:, g // PER, O1 * (g % PER):O1 * (g % PER) + O1]

        def evacuate(copy, banks, done):
            for b in banks:
                n = min(PER, NG - b * PER)
                last = copy(sums[:, b * PER:b * PER + n, :].rearrange("p g o -> p (g o)"), acc[:, b, 0:n * O1])
            last.then_inc(done, 1)

        block = ctx.enter_context(nc.Block())

        @block.sync
        def _(sp):
            def load_src(c, tile, loaded):
                rows = s_dram[:, bass.ds(c * CH, CH)].unsqueeze(0).broadcast_to([P, H, CH])
                sp.dma_start(tile[:, :, :], rows).then_inc(loaded, 16)

            def chunk(c, last):
                if not last:
                    sp.wait_ge(s_step, H * (PAIRS * c + 2))
                    load_src(c + 1, src_head, s_head)
                sp.dma_start(xrow_v, x_v[c]).then_inc(s_x, 16)
                if not last:
                    sp.wait_ge(s_step, H * (PAIRS * c + PAIRS))
                    load_src(c + 1, src_rest, s_rest)
                sp.wait_ge(s_post, STEPS * (c + 2))
                sp.dma_start(x1_v[c], xrow_v).then_inc(s_out, 16)
                sp.wait_ge(s_out, 16 * c + 16)
                sp.sem_inc(s_carry, 1)

            load_src(0, src_head, s_head)
            load_src(0, src_rest, s_rest)
            with sp.Fori(0, NC - 1) as c:
                chunk(c, False)
            chunk(NC - 1, True)

        @block.gpsimd
        def _(pool):
            def load(c, l):
                pool.dma_start(araw[l % 2][:, :, :], adj_v[c, l]).then_inc(s_adj[l % 2], 16)

            def reload(c, l):
                pool.wait_ge(s_turn, PAIRS * c + PPL * (l + 1))
                if l + 2 < LOADS:
                    load(c, l + 2)
                else:
                    load(c + 1, l + 2 - LOADS)

            def bc(ap, n):
                return ap.unsqueeze(2).broadcast_to([P, n, O])

            def post(c, k):
                Es, Fs = sums[:, 0:TH, 0:O], sums[:, TH:2 * TH, 0:O]
                at = bass.ds(c * TILES, TILES)
                tt = nc.gpsimd.tensor_tensor
                if k == 0:
                    pool.wait_ge(s_sumA, c + 2)
                    pool.wait_ge(s_sumD, c + 2)
                    pool.wait_ge(s_den, 4 * c + 4)
                    f = sums[:, TH:2 * TH, 0:O].rearrange("p (t h) o -> p t h o", t=TILES)[:, :, EXPLICIT:H, :]
                    af = sums[:, 2 * TH:NG, 0:O].rearrange("p (t h) o -> p t h o", t=TILES)
                    tt(f, af, f, ALU.subtract).then_inc(s_post, 1)
                elif k == 1:
                    tt(Es, Es, bc(cE[:, at, :].rearrange("p t h -> p (t h)"), TH), ALU.mult).then_inc(s_post, 1)
                elif k == 2:
                    pool.wait_ge(s_post, STEPS * (c + 1) + 1)
                    tt(Fs, Fs, bc(cF[:, at, :].rearrange("p t h -> p (t h)"), TH), ALU.mult).then_inc(s_post, 1)
                elif k == 3:
                    pool.wait_ge(s_post, STEPS * (c + 1) + 3)
                    tt(Es, Es, Fs, ALU.add).then_inc(s_post, 1)
                elif k == 4:
                    pool.wait_ge(s_post, STEPS * (c + 1) + 4)
                    tt(Es, Es, bc(rden[:, :], TH), ALU.mult).then_inc(s_post, 1)
                else:
                    pool.wait_ge(s_post, STEPS * (c + 1) + 5)
                    pool.wait_ge(s_x, 16 * c + 16)
                    tt(xrow[:, :, :], xrow[:, :, :], Es, ALU.add).then_inc(s_post, 1)

            def finish(c, reload_too):
                for l in range(4):
                    if reload_too:
                        reload(c + 1, l)
                    for k in {1: (0, 1), 2: (2, 3), 3: (4, 5)}.get(l, ()):
                        post(c, k)

            pool.sem_inc(s_post, STEPS)
            make_identity(nc, pool, ident, s_id)
            load(0, 0)
            load(0, 1)
            for l in range(4):
                reload(0, l)
            with pool.Fori(0, NC - 1) as c:
                for l in range(4, LOADS):
                    reload(c, l)
                finish(c, True)
            for l in range(4, LOADS - 2):
                reload(NC - 1, l)
            finish(NC - 1, False)

        @block.scalar
        def _(act):
            def pair(c, p, tile):
                for h in range(H):
                    u = H * (PAIRS * c + p) + h
                    slot = h % 2
                    if not (isinstance(u, int) and u < 2):
                        act.wait_ge(s_B, u - 1)
                    for jj in range(2):
                        jb = 2 * p + jj
                        last = nc.scalar.activation(step[slot][:, jj, :], tile[:, h, :], ACT.Sigmoid,
                                                    bias=dsharp[:, jb, h:h + 1], scale=SHARP)
                    last.then_inc(s_step, 1)

            def sums_out(c):
                act.wait_ge(s_used, PAIRS * (c + 1))
                act.wait_ge(s_post, STEPS * (c + 1))
                evacuate(lambda o, i: nc.scalar.activation(o, i, ACT.Copy), range(NBA), s_sumA)

            act.sem_inc(s_sumA, 1)
            act.wait_ge(s_head, 16)
            pair(0, 0, src_head)
            pair(0, 1, src_head)
            with act.Fori(0, NC - 1) as c:
                act.wait_ge(s_rest, 16 * c + 16)
                for p in range(2, PAIRS):
                    pair(c, p, src_rest)
                act.wait_ge(s_head, 16 * c + 32)
                pair(c + 1, 0, src_head)
                sums_out(c)
                pair(c + 1, 1, src_head)
            act.wait_ge(s_rest, 16 * NC)
            for p in range(2, PAIRS):
                pair(NC - 1, p, src_rest)
            sums_out(NC - 1)

        @block.vector
        def _(dve):
            def pair(c, p):
                q = PAIRS * c + p
                k = p % 2
                dve.wait_ge(s_turn, q + 1)
                if not (isinstance(q, int) and q < 2):
                    dve.wait_ge(s_used, q - 1)
                nc.vector.tensor_scalar(A[k][:, :, :], turned[k][:, :, :], 0.0, None, ALU.is_gt).then_inc(s_A, 1)
                dve.wait_ge(s_A, q + 1)
                for h in range(H + 1):
                    if h < H:
                        dve.wait_ge(s_step, H * q + h + 1)
                        nc.vector.tensor_tensor(B[k][h][:, :, :], step[h % 2][:, :, :], A[k][:, :, :],
                                                ALU.mult).then_inc(s_B, 1)
                    if 0 < h <= EXPLICIT:
                        dve.wait_ge(s_B, H * q + h)
                        last = nc.vector.tensor_tensor(C[k][h - 1][:, :, :], A[k][:, :, :], B[k][h - 1][:, :, :],
                                                       ALU.subtract)
                        last.then_inc(s_masks, 1)

            def sums_out(c):
                dve.wait_ge(s_used, PAIRS * (c + 1))
                dve.wait_ge(s_post, STEPS * (c + 1))
                evacuate(lambda o, i: nc.vector.tensor_copy(o, i), range(NBA, NB), s_sumD)
                dve.wait_ge(s_sumD, c + 2)
                dve.wait_ge(s_sumA, c + 2)
                at = bass.ds(c * TILES, TILES)
                four = "p (t h) -> p t h"
                Ed, Fd = sums[:, 0:TH, O], sums[:, TH:2 * TH, O]
                fd = Fd.rearrange(four, t=TILES)[:, :, EXPLICIT:H]
                af = sums[:, 2 * TH:NG, O].rearrange(four, t=TILES)
                d0 = den[:, 0, :].rearrange(four, t=TILES)
                d1 = den[:, 1, :].rearrange(four, t=TILES)
                nc.vector.tensor_tensor(fd, af, fd, ALU.subtract)
                nc.vector.tensor_tensor(d0, Ed.rearrange(four, t=TILES), cE[:, at, :], ALU.mult).then_inc(s_den, 1)
                dve.wait_ge(s_den, 4 * c + 1)
                nc.vector.tensor_tensor(d1, Fd.rearrange(four, t=TILES), cF[:, at, :], ALU.mult).then_inc(s_den, 1)
                dve.wait_ge(s_den, 4 * c + 2)
                nc.vector.tensor_tensor(den[:, 0, :], den[:, 0, :], den[:, 1, :], ALU.add).then_inc(s_den, 1)
                dve.wait_ge(s_den, 4 * c + 3)
                nc.vector.reciprocal(rden[:, :], den[:, 0, :]).then_inc(s_den, 1)

            dve.sem_inc(s_sumD, 1)
            pair(0, 0)
            pair(0, 1)
            with dve.Fori(0, NC - 1) as c:
                for p in range(2, PAIRS):
                    pair(c, p)
                pair(c + 1, 0)
                sums_out(c)
                pair(c + 1, 1)
            for p in range(2, PAIRS):
                pair(NC - 1, p)
            sums_out(NC - 1)

        @block.tensor
        def _(pe):
            def turn(c, p):
                k = p % 2
                if p % PPL == 0:
                    l = p // PPL
                    pe.wait_ge(s_adj[l % 2], 16 * (LOADS // 2 * c + l // 2 + 1))
                q = PAIRS * c + p
                if not (isinstance(q, int) and q < 2):
                    pe.wait_ge(s_A, q - 1)
                for jj in range(2):
                    col = (2 * (p % PPL) + jj) * P
                    for t in range(TILES):
                        last = nc.tensor.transpose(turned[k][:, jj, t * P:(t + 1) * P],
                                                   araw[p // PPL % 2][:, t, col:col + P], ident[:, :])
                last.then_inc(s_turn, 1)

            def products(c, p, open_banks):
                k = p % 2
                pe.wait_ge(s_masks, EXPLICIT * (PAIRS * c + p + 1))
                if EXPLICIT < H:
                    pe.wait_ge(s_B, H * (PAIRS * c + p + 1))
                if p == 0:
                    pe.wait_ge(s_sumA, c + 1)
                    pe.wait_ge(s_sumD, c + 1)
                for jj in range(2):
                    jb = 2 * p + jj
                    for t in range(TILES):
                        def add(mask, term, h, g):
                            for part in range(2):
                                opens = jb == 0 and part == 0 and g // PER not in open_banks
                                x = nc.tensor.matmul(slot_of(g), mask[:, jj, t * P:(t + 1) * P],
                                                     V[:, jb, 2 * term + part, h, :], start=opens,
                                                     stop=(jb == NT - 1 and part == 1), skip_group_check=True)
                                if opens:
                                    open_banks.add(g // PER)
                            return x

                        for h in range(H):
                            g = t * H + h
                            last = add(B[k][h], 0, h, g)
                            if h < EXPLICIT:
                                last = add(C[k][h], 1, h, TH + g)
                            else:
                                last = add(B[k][h], 1, h, TH + g)
                        for h in range(EXPLICIT, H):
                            last = add(A[k], 1, h, 2 * TH + t * IMPLICIT + h - EXPLICIT)
                last.then_inc(s_used, 1)

            pe.wait_ge(s_id, 2)
            turn(0, 0)
            turn(0, 1)
            with pe.Fori(0, NC - 1) as c:
                open_banks = set()
                for p in range(PAIRS):
                    products(c, p, open_banks)
                    turn(c, p + 2) if p + 2 < PAIRS else turn(c + 1, p + 2 - PAIRS)
            open_banks = set()
            for p in range(PAIRS):
                products(NC - 1, p, open_banks)
                if p + 2 < PAIRS:
                    turn(NC - 1, p + 2)


def mixture(nc, x1_dram, gamma, beta, wr, br, w1, b1, w2, b2, out):
    N, D = x1_dram.shape
    NE, _, HID = w1.shape
    DO = w2.shape[2]
    NC, KD, M = N // CH, D // P, HID // P
    NT_C = NE * M
    RING = 4
    AHEAD = 2
    ROWS = NE * M + 2 * KD
    with ExitStack() as ctx:
        def sb(name, shape, dt=F32):
            return ctx.enter_context(nc.sbuf_tensor(name, shape, dt))

        def sem(name):
            return ctx.enter_context(nc.semaphore(name))

        w1h = sb("f_w1h", [P, NE, KD, HID], F32R)
        w1l = sb("f_w1l", [P, NE, KD, HID], F32R)
        w2h = sb("f_w2h", [P, NE, M, DO], F32R)
        w2l = sb("f_w2l", [P, NE, M, DO], F32R)
        w1raw = sb("f_w1raw", [P, KD, HID])
        w2raw = sb("f_w2raw", [P, M, DO])
        ident = sb("f_ident", [P, P])
        rows = sb("f_rows", [ROWS, P])
        cols = sb("f_cols", [P, ROWS])
        wrs = sb("f_wr", [P, KD, NE])
        brow = sb("f_br", [P, NE])
        b2s = sb("f_b2", [NE, DO])
        iota = sb("f_iota", [P, NE])
        eps = sb("f_eps", [P, 1])
        xs = [sb(f"f_xs{k}", [P, TILES, D]) for k in range(2)]
        nrm = sb("f_nrm", [P, TILES, D])
        stats = sb("f_stats", [P, TILES, 6])
        meanvar = sb("f_meanvar", [P, TILES, 2])
        std = sb("f_std", [P, TILES])
        rstd = sb("f_rstd", [P, TILES])
        xT = sb("f_xT", [P, KD, CH])
        xTh = [sb(f"f_xTh{k}", [P, KD, CH], F32R) for k in range(2)]
        xTl = [sb(f"f_xTl{k}", [P, KD, CH], F32R) for k in range(2)]
        logits = sb("f_logits", [P, TILES, NE])
        best = sb("f_best", [P, TILES, 8])
        where = sb("f_where", [P, TILES, 8], U32)
        wheref = sb("f_wheref", [P, TILES, 2])
        gap = sb("f_gap", [P, TILES])
        egap = sb("f_egap", [P, TILES])
        onep = sb("f_onep", [P, TILES])
        wtop = sb("f_wtop", [P, 2, TILES])
        pick = sb("f_pick", [P, 2, TILES, NE])
        gates = [sb(f"f_gates{k}", [P, TILES, NE]) for k in range(2)]
        gatesT = sb("f_gatesT", [NE, CH])
        hid = [sb(f"f_hid{k}", [P, CH]) for k in range(RING)]
        hidh = [sb(f"f_hidh{k}", [P, CH], F32R) for k in range(RING)]
        hidl = [sb(f"f_hidl{k}", [P, CH], F32R) for k in range(RING)]
        psH = [ctx.enter_context(nc.psum_tensor(f"f_psH{k}", [P, CH], F32)) for k in range(AHEAD)]
        psY = [ctx.enter_context(nc.psum_tensor(f"f_psY{k}", [P, TILES, DO], F32)) for k in range(2)]
        psM = ctx.enter_context(nc.psum_tensor("f_psM", [P, CH], F32))

        s_row = sem("f_rows_loaded")
        s_small = sem("f_small_loaded")
        s_w1raw = sem("f_w1_loaded")
        s_w2raw = sem("f_w2_loaded")
        s_w1 = sem("f_w1_split_steps")
        s_w2 = sem("f_w2_split_steps")
        s_id = sem("f_identity")
        s_const = sem("f_const")
        s_colps = sem("f_cols_in_psum")
        s_cols = sem("f_cols_ready")
        s_x = [sem("f_x1_loaded0"), sem("f_x1_loaded1")]
        s_st = [sem("f_out_stored0"), sem("f_out_stored1")]
        s_stats1 = sem("f_stats1")
        s_aggr1 = sem("f_aggr1")
        s_std1 = sem("f_std1")
        s_rstd1 = sem("f_rstd1")
        s_nrm1 = sem("f_norm1")
        s_stats2 = sem("f_stats2")
        s_aggr2 = sem("f_aggr2")
        s_std2 = sem("f_std2")
        s_rstd2 = sem("f_rstd2")
        s_nrm2 = sem("f_norm2")
        s_tps = sem("f_xT_in_psum")
        s_xT = sem("f_xT_ready")
        s_xh = sem("f_xT_hi_ready")
        s_xl = sem("f_xT_lo_ready")
        s_lgps = sem("f_logits_in_psum")
        s_lg = sem("f_logits_ready")
        s_best = sem("f_best_ready")
        s_where = sem("f_where_ready")
        s_gap = sem("f_gap_ready")
        s_egap = sem("f_exp_gap_ready")
        s_g = sem("f_gate_steps")
        s_gates = sem("f_gates_ready")
        s_gtps = sem("f_gatesT_in_psum")
        s_gt = sem("f_gatesT_ready")
        s_b2ps = sem("f_b2_in_psum")
        s_b2 = sem("f_b2_added")
        s_h = sem("f_hidden_in_psum")
        s_gelu = sem("f_gelu_ready")
        s_hh = sem("f_hidden_hi")
        s_hl = sem("f_hidden_lo")
        s_y = sem("f_expert_in_psum")
        s_acc = sem("f_expert_added")
        s_carry = sem("f_wait_carrier")

        x1_v = x1_dram.rearrange("(c t p) d -> c p t d", p=P, t=TILES)
        out_v = out.rearrange("(c t p) d -> c p t d", p=P, t=TILES)
        block = ctx.enter_context(nc.Block())

        def loop(eng, body):
            with eng.Fori(0, NC // 2 - 1) as i:
                for slot in range(2):
                    body(i, slot, False)
            body(NC // 2 - 1, 0, False)
            body(NC // 2 - 1, 1, True)

        @block.sync
        def _(sp):
            sp.dma_start(rows[0:NE * M, :], b1.rearrange("e (m p) -> (e m) p", p=P)).then_inc(s_row, 16)
            sp.dma_start(rows[NE * M:NE * M + KD, :], gamma.rearrange("(k p) -> k p", p=P)).then_inc(s_row, 16)
            sp.dma_start(rows[NE * M + KD:ROWS, :], beta.rearrange("(k p) -> k p", p=P)).then_inc(s_row, 16)
            sp.dma_start(xs[0][:, :, :], x1_v[0]).then_inc(s_x[0], 16)
            sp.dma_start(wrs[:, :, :], wr.rearrange("(k p) e -> p k e", p=P)).then_inc(s_small, 16)
            sp.dma_start(brow[:, :], br.rearrange("(u e) -> u e", u=1).broadcast_to([P, NE])).then_inc(s_small, 16)
            sp.dma_start(b2s[:, :], b2).then_inc(s_small, 16)
            for e in range(NE):
                if e:
                    sp.wait_ge(s_w1, 2 * e)
                sp.dma_start(w1raw[:, :, :], w1[e].rearrange("(k p) n -> p k n", p=P)).then_inc(s_w1raw, 16)
                if e:
                    sp.wait_ge(s_w2, 2 * e)
                sp.dma_start(w2raw[:, :, :], w2[e].rearrange("(m p) n -> p m n", p=P)).then_inc(s_w2raw, 16)
            sp.dma_start(xs[1][:, :, :], x1_v[1]).then_inc(s_x[1], 16)

            def store(c, slot):
                sp.wait_ge(s_acc, NE * c + NE)
                sp.dma_start(out_v[c], xs[slot][:, :, :]).then_inc(s_st[slot], 16)

            with sp.Fori(0, NC // 2 - 1) as i:
                for slot in range(2):
                    store(2 * i + slot, slot)
                    sp.wait_ge(s_st[slot], 16 * i + 16)
                    sp.dma_start(xs[slot][:, :, :], x1_v[2 * i + slot + 2]).then_inc(s_x[slot], 16)
            store(NC - 2, 0)
            store(NC - 1, 1)
            for slot in range(2):
                sp.wait_ge(s_st[slot], 16 * (NC // 2))

        @block.gpsimd
        def _(pool):
            make_identity(nc, pool, ident, s_id)
            nc.gpsimd.memset(eps[:, :], LN_EPS).then_inc(s_const, 1)
            nc.gpsimd.iota(iota[:, :], pattern=[[1, NE]], base=0, channel_multiplier=0,
                           allow_small_or_imprecise_dtypes=True).then_inc(s_const, 1)
            for e in range(NE):
                for raw, hi, lo, loaded, split in ((w1raw, w1h, w1l, s_w1raw, s_w1),
                                                   (w2raw, w2h, w2l, s_w2raw, s_w2)):
                    pool.wait_ge(loaded, 16 * (e + 1))
                    nc.gpsimd.tensor_copy(hi[:, e, :, :], raw[:, :, :]).then_inc(split, 1)
                    pool.wait_ge(split, 2 * e + 1)
                    nc.gpsimd.tensor_tensor(lo[:, e, :, :], raw[:, :, :], hi[:, e, :, :].bitcast(F32),
                                            ALU.subtract).then_inc(split, 1)

        @block.scalar
        def _(act):
            def root(c, slot, aggr, done):
                act.wait_ge(aggr, c + 1)
                nc.scalar.activation(std[:, :], meanvar[:, :, 1], ACT.Sqrt, bias=eps[:, 0:1]).then_inc(done, 1)

            def turned(c, slot, k):
                g = NE * M + k
                act.wait_ge(s_tps, KD * c + k + 1)
                nc.scalar.activation(xT[:, k, :], psM[:, :], ACT.Identity, bias=cols[:, g + KD:g + KD + 1],
                                     scale=cols[:, g:g + 1]).then_inc(s_xT, 1)

            def exp_gap(c, slot):
                act.wait_ge(s_gap, c + 1)
                nc.scalar.activation(egap[:, :], gap[:, :], ACT.Exp).then_inc(s_egap, 1)

            def gates_turned(c, slot):
                act.wait_ge(s_gtps, c + 1)
                nc.scalar.activation(gatesT[:, :], psM[0:NE, :], ACT.Copy).then_inc(s_gt, 1)

            def prepare(n, i, slot):
                c = 2 * i + slot
                if n == 9:
                    root(c, slot, s_aggr1, s_std1)
                elif n == 12:
                    root(c, slot, s_aggr2, s_std2)
                elif n == 16:
                    turned(c, slot, 0)
                elif n == 18:
                    turned(c, slot, 1)
                elif n == 22:
                    exp_gap(c, slot)
                elif n == 26:
                    gates_turned(c, slot)

            def body(i, slot, last):
                c = 2 * i + slot
                for n in range(NT_C):
                    act.wait_ge(s_h, NT_C * c + n + 1)
                    nc.scalar.activation(hid[n % RING][:, :], psH[n % AHEAD][:, :], ACT.Gelu,
                                         bias=cols[:, n:n + 1]).then_inc(s_gelu, 1)
                    if not last:
                        prepare(n, i + slot, 1 - slot)

            act.wait_ge(s_const, 2)
            act.wait_ge(s_cols, 1)
            for n in range(NT_C):
                prepare(n, 0, 0)
            loop(act, body)

        @block.vector
        def _(dve):
            tt, ts = nc.vector.tensor_tensor, nc.vector.tensor_scalar

            def norm(c, src, dst, stats_done, aggr_done, std_done, rstd_done, norm_done, part):
                if part == 0:
                    for t in range(TILES):
                        last = nc.vector.bn_stats(stats[:, t, :], src[:, t, :])
                    last.then_inc(stats_done, 1)
                    dve.wait_ge(stats_done, c + 1)
                    dve.sem_inc(s_carry, 1)
                    for t in range(TILES):
                        last = nc.vector.bn_aggr(meanvar[:, t, :], stats[:, t, :])
                    last.then_inc(aggr_done, 1)
                else:
                    dve.wait_ge(std_done, c + 1)
                    nc.vector.reciprocal(rstd[:, :], std[:, :]).then_inc(rstd_done, 1)
                    dve.wait_ge(rstd_done, c + 1)
                    for t in range(TILES):
                        last = ts(dst[:, t, :], src[:, t, :], meanvar[:, t, 0:1], rstd[:, t:t + 1],
                                  ALU.subtract, ALU.mult)
                    last.then_inc(norm_done, 1)

            def norm1(c, slot, part):
                norm(c, xs[slot], nrm, s_stats1, s_aggr1, s_std1, s_rstd1, s_nrm1, part)

            def norm2(c, slot, part):
                norm(c, nrm, nrm, s_stats2, s_aggr2, s_std2, s_rstd2, s_nrm2, part)

            def split_xT(c, slot):
                dve.wait_ge(s_xT, KD * (c + 1))
                nc.vector.tensor_copy(xTh[slot][:, :, :], xT[:, :, :]).then_inc(s_xh, 1)
                dve.wait_ge(s_xh, c + 1)
                tt(xTl[slot][:, :, :], xT[:, :, :], xTh[slot][:, :, :].bitcast(F32), ALU.subtract).then_inc(s_xl, 1)

            def top2(c, slot):
                dve.wait_ge(s_lgps, c + 1)
                tt(logits[:, :, :], psM[:, 0:TILES * NE].rearrange("p (t e) -> p t e", t=TILES),
                   brow[:, :].unsqueeze(1).broadcast_to([P, TILES, NE]), ALU.add).then_inc(s_lg, 1)
                dve.wait_ge(s_lg, c + 1)
                dve.sem_inc(s_carry, 1)
                for t in range(TILES):
                    last = nc.vector.max(best[:, t, :], logits[:, t, :])
                last.then_inc(s_best, 1)
                dve.wait_ge(s_best, c + 1)
                dve.sem_inc(s_carry, 1)
                for t in range(TILES):
                    last = nc.vector.max_index(where[:, t, :], best[:, t, :], logits[:, t, :])
                last.then_inc(s_where, 1)
                tt(gap[:, :], best[:, :, 1], best[:, :, 0], ALU.subtract).then_inc(s_gap, 1)

            def make_gates(c, slot):
                dve.wait_ge(s_where, c + 1)
                nc.vector.tensor_copy(wheref[:, :, :], where[:, :, 0:2]).then_inc(s_g, 1)
                dve.wait_ge(s_egap, c + 1)
                ts(onep[:, :], egap[:, :], 1.0, None, ALU.add).then_inc(s_g, 1)
                dve.wait_ge(s_g, 6 * c + 2)
                nc.vector.reciprocal(wtop[:, 0, :], onep[:, :]).then_inc(s_g, 1)
                dve.wait_ge(s_g, 6 * c + 3)
                tt(wtop[:, 1, :], egap[:, :], wtop[:, 0, :], ALU.mult).then_inc(s_g, 1)
                dve.wait_ge(s_g, 6 * c + 4)
                for k in range(2):
                    for t in range(TILES):
                        last = ts(pick[:, k, t, :], iota[:, :], wheref[:, t, k:k + 1], wtop[:, k, t:t + 1],
                                  ALU.is_equal, ALU.mult)
                    last.then_inc(s_g, 1)
                dve.wait_ge(s_g, 6 * c + 6)
                tt(gates[slot][:, :, :], pick[:, 0, :, :], pick[:, 1, :, :], ALU.add).then_inc(s_gates, 1)

            def add_b2(c, slot, half):
                dve.wait_ge(s_b2ps, 2 * c + half + 1)
                two = xs[slot][:, 2 * half:2 * half + 2, :]
                tt(two, two, psM[:, :].rearrange("p (t d) -> p t d", t=2), ALU.add).then_inc(s_b2, 1)

            def prepare(n, i, slot):
                c = 2 * i + slot
                if n == 8:
                    dve.wait_ge(s_x[slot], 16 * i + 16)
                    norm1(c, slot, 0)
                elif n == 10:
                    norm1(c, slot, 1)
                    dve.wait_ge(s_nrm1, c + 1)
                    norm2(c, slot, 0)
                elif n == 13:
                    norm2(c, slot, 1)
                elif n == 19:
                    split_xT(c, slot)
                elif n == 21:
                    top2(c, slot)
                elif n == 23:
                    make_gates(c, slot)
                elif n == 28:
                    add_b2(c, slot, 0)
                elif n == 30:
                    add_b2(c, slot, 1)

            def split(c, n):
                g = NT_C * c + n
                k = n % RING
                dve.wait_ge(s_gelu, g + 1)
                nc.vector.tensor_copy(hidh[k][:, :], hid[k][:, :]).then_inc(s_hh, 1)
                dve.wait_ge(s_hh, g + 1)
                tt(hidl[k][:, :], hid[k][:, :], hidh[k][:, :].bitcast(F32), ALU.subtract).then_inc(s_hl, 1)

            def accumulate(c, slot, e):
                dve.wait_ge(s_y, NE * c + e + 1)
                if e:
                    dve.wait_ge(s_acc, NE * c + e)
                else:
                    dve.wait_ge(s_b2, 2 * c + 2)
                for t in range(TILES):
                    last = nc.vector.scalar_tensor_tensor(out=xs[slot][:, t, :], in0=psY[e % 2][:, t, :],
                                                          scalar=gates[slot][:, t, e:e + 1],
                                                          in1=xs[slot][:, t, :], op0=ALU.mult, op1=ALU.add)
                last.then_inc(s_acc, 1)

            def body(i, slot, last):
                c = 2 * i + slot
                for n in range(3, NT_C):
                    split(c, n)
                    if n % M == 2:
                        accumulate(c, slot, n // M - 1)
                    if not last:
                        prepare(n, i + slot, 1 - slot)
                if not last:
                    for n in range(3):
                        split(c + 1, n)
                accumulate(c, slot, NE - 1)

            dve.wait_ge(s_colps, 1)
            nc.vector.tensor_copy(cols[:, :], psM[:, 0:ROWS]).then_inc(s_cols, 1)
            dve.wait_ge(s_small, 48)
            dve.wait_ge(s_const, 2)
            for n in range(NT_C):
                prepare(n, 0, 0)
            for n in range(3):
                split(0, n)
            loop(dve, body)

        @block.tensor
        def _(pe):
            def turn(c, slot, k):
                pe.wait_ge(s_nrm2, c + 1)
                if k:
                    pe.wait_ge(s_xT, KD * c + k)
                for t in range(TILES):
                    last = nc.tensor.transpose(psM[:, t * P:(t + 1) * P], nrm[:, t, k * P:(k + 1) * P], ident[:, :])
                last.then_inc(s_tps, 1)

            def route(c, slot):
                pe.wait_ge(s_xT, KD * (c + 1))
                for t in range(TILES):
                    for k in range(KD):
                        last = nc.tensor.matmul(psM[:, t * NE:(t + 1) * NE], xT[:, k, t * P:(t + 1) * P],
                                                wrs[:, k, :], start=(k == 0), stop=(k == KD - 1))
                last.then_inc(s_lgps, 1)

            def turn_gates(c, slot):
                pe.wait_ge(s_gates, c + 1)
                for t in range(TILES):
                    last = nc.tensor.transpose(psM[0:NE, t * P:(t + 1) * P], gates[slot][:, t, :], ident[:, :])
                last.then_inc(s_gtps, 1)

            def bias2(c, slot, half):
                pe.wait_ge(s_gt, c + 1)
                if half:
                    pe.wait_ge(s_b2, 2 * c + 1)
                for t in range(2):
                    at = (2 * half + t) * P
                    last = nc.tensor.matmul(psM[:, t * DO:(t + 1) * DO], gatesT[:, at:at + P], b2s[:, :],
                                            start=True, stop=True)
                last.then_inc(s_b2ps, 1)

            def prepare(n, i, slot):
                c = 2 * i + slot
                if n == 15:
                    turn(c, slot, 0)
                elif n == 17:
                    turn(c, slot, 1)
                elif n == 19:
                    route(c, slot)
                elif n == 25:
                    turn_gates(c, slot)
                elif n == 27:
                    bias2(c, slot, 0)
                elif n == 29:
                    bias2(c, slot, 1)

            def hidden(c, slot, n):
                e, m = n // M, n % M
                if m == 0:
                    pe.wait_ge(s_w1, 2 * e + 2)
                if n == 0:
                    pe.wait_ge(s_xl, c + 1)
                if not (isinstance(c, int) and c == 0 and n < AHEAD):
                    pe.wait_ge(s_gelu, NT_C * c + n - AHEAD + 1)
                products = [(w, x, k) for k in range(KD) for w, x in ((w1h, xTh), (w1h, xTl), (w1l, xTh))]
                for j, (w, x, k) in enumerate(products):
                    last = nc.tensor.matmul(psH[n % AHEAD][:, :], w[:, e, k, m * P:(m + 1) * P], x[slot][:, k, :],
                                            start=(j == 0), stop=(j == len(products) - 1))
                last.then_inc(s_h, 1)

            def second(c, n):
                e, m = n // M, n % M
                pe.wait_ge(s_hl, NT_C * c + n + 1)
                if m == 0:
                    pe.wait_ge(s_w2, 2 * e + 2)
                k = n % RING
                for t in range(TILES):
                    for j, (h, w) in enumerate(((hidh, w2h), (hidh, w2l), (hidl, w2h))):
                        last = nc.tensor.matmul(psY[e % 2][:, t, :], h[k][:, t * P:(t + 1) * P], w[:, e, m, :],
                                                start=(m == 0 and j == 0 and t % 2 == 0),
                                                stop=(m == M - 1 and j == 2), skip_group_check=True)
                if m == M - 1:
                    last.then_inc(s_y, 1)

            def body(i, slot, last):
                c = 2 * i + slot
                for n in range(NT_C):
                    if n + AHEAD < NT_C:
                        hidden(c, slot, n + AHEAD)
                    elif not last:
                        hidden(c + 1, 1 - slot, n + AHEAD - NT_C)
                    second(c, n)
                    if not last:
                        prepare(n, i + slot, 1 - slot)

            pe.wait_ge(s_id, 2)
            pe.wait_ge(s_row, 48)
            nc.tensor.transpose(psM[:, 0:ROWS], rows[:, :], ident[0:ROWS, 0:ROWS]).then_inc(s_colps, 1)
            pe.wait_ge(s_cols, 1)
            pe.wait_ge(s_small, 48)
            for n in range(NT_C):
                prepare(n, 0, 0)
            for n in range(AHEAD):
                hidden(0, 0, n)
            loop(pe, body)


def layer(nc, x, adj, gnn_w, gnn_a, gamma, beta, wr, br, w1, b1, w2, b2, out, only_gnn=False):
    N, D = x.shape
    H, _, O = gnn_w.shape
    NT = N // P
    xt_dram = nc.dram_tensor("xt_scratch", [N, H * O], F32, kind="Internal").ap()
    s_dram = nc.dram_tensor("src_scratch", [H, N], F32, kind="Internal").ap()
    x1_dram = out if only_gnn else nc.dram_tensor("x1_scratch", [N, D], F32, kind="Internal").ap()
    with ExitStack() as graph:
        def sb(name, shape, dt=F32):
            return graph.enter_context(nc.sbuf_tensor(name, shape, dt))

        V = sb("V", [P, NT, 4, H, O + 1], F16)
        keep = {name: sb(name, [P, NT, H]) for name in ("cE", "cF", "dsharp")}
        with ExitStack() as rows:
            for name in ("E", "F"):
                keep[name] = rows.enter_context(nc.sbuf_tensor(name, [P, NT, H], F32))
            project(nc, x, gnn_w, gnn_a, xt_dram, s_dram, keep)
            split_rows(nc, xt_dram, V, keep, N, H, O)
        attend(nc, x, adj, s_dram, x1_dram, V, keep, H, O)
    if not only_gnn:
        mixture(nc, x1_dram, gamma, beta, wr, br, w1, b1, w2, b2, out)


_INS = ["x", "adj", "L0_gnn_W", "L0_gnn_a", "L0_ffn_gamma", "L0_ffn_beta", "L0_ffn_Wr", "L0_ffn_br",
        "L0_ffn_W1", "L0_ffn_b1", "L0_ffn_W2", "L0_ffn_b2"]


def kernel(**inputs):
    import numpy as _np
    import concourse.bacc as _bacc
    from concourse import mybir as _mybir
    from concourse.bass_utils import run_bass_kernel_spmd as _run

    nc = _bacc.Bacc("TRN2", target_bir_lowering=False, num_devices=1)
    arrays, args = {}, []
    for name in _INS:
        a = _np.ascontiguousarray(inputs[name])
        arrays[f"in_{name}"] = a
        args.append(nc.dram_tensor(f"in_{name}", a.shape, _mybir.dt.from_np(a.dtype), kind="ExternalInput").ap())
    out = nc.dram_tensor("out", inputs["x"].shape, _mybir.dt.float32, kind="ExternalOutput").ap()
    layer(nc, *args, out)
    r = _run(nc, [arrays], core_ids=[0])
    return r.results[0]["out"]
```

```python
from contextlib import ExitStack

import concourse.bass as bass
from concourse import mybir

F32 = mybir.dt.float32
F32R = mybir.dt.float32r
BF16 = mybir.dt.bfloat16
F16 = mybir.dt.float16
U32 = mybir.dt.uint32
ALU = mybir.AluOpType
ACT = mybir.ActivationFunctionType
AX = mybir.AxisListType.X
RMAX = bass.bass_isa.ReduceOp.max

P = 128
SLOPE = 0.2
LN_EPS = 1e-5
SHARP = 2.0 ** 60
HALF_TOP = 2.0 ** 14

TILES = 4
CH = TILES * P


def make_identity(nc, pool, ident, written):
    nc.gpsimd.memset(ident[:, :], 0.0).then_inc(written, 1)
    pool.wait_ge(written, 1)
    nc.gpsimd.affine_select(out=ident[:, :], in_=ident[:, :], compare_op=ALU.not_equal, fill=1.0,
                            base=0, pattern=[[-1, P]], channel_multiplier=1).then_inc(written, 1)


def past(c, n):
    return not isinstance(c, int) or c >= n


def turns(eng, chunks, ring, step):
    for slot in range(ring):
        step(0, slot)
    with eng.Fori(1, chunks // ring) as i:
        for slot in range(ring):
            step(i, slot)


def project(nc, x, gnn_w, gnn_a, xt_dram, s_dram, keep):
    N, D = x.shape
    H, _, O = gnn_w.shape
    NT, NC, KD = N // P, N // CH, D // P
    RING = 4
    W1 = H * O + 2 * H
    cE, cF, dsharp, ndst, E, F = (keep[name] for name in ("cE", "cF", "dsharp", "ndst", "E", "F"))
    with ExitStack() as ctx:
        def sb(name, shape, dt=F32):
            return ctx.enter_context(nc.sbuf_tensor(name, shape, dt))

        def ps(name, shape, dt=F32):
            return ctx.enter_context(nc.psum_tensor(name, shape, dt))

        def sem(name):
            return ctx.enter_context(nc.semaphore(name))

        ident = sb("p_ident", [P, P])
        wext = sb("p_wext", [P, KD, W1])
        wprod = sb("p_wprod", [P, H, 2, O])
        arow = sb("p_arow", [P, H, 2, O])
        eps = sb("p_eps", [P, 1])
        xin = [sb(f"p_xin{k}", [P, TILES, D]) for k in range(RING)]
        xn = [sb(f"p_xn{k}", [P, TILES, D]) for k in range(2)]
        stats = [sb(f"p_stats{k}", [P, TILES, 6]) for k in range(2)]
        meanvar = [sb(f"p_meanvar{k}", [P, TILES, 2]) for k in range(2)]
        std = [sb(f"p_std{k}", [P, TILES]) for k in range(2)]
        rstd = [sb(f"p_rstd{k}", [P, TILES]) for k in range(2)]
        xnT = [sb(f"p_xnT{k}", [P, KD, CH]) for k in range(2)]
        xto = [sb(f"p_xto{k}", [P, TILES, W1]) for k in range(2)]
        srcdst = sb("p_srcdst", [P, NT, 2 * H])
        vpart = sb("p_vpart", [P, NC])
        top = sb("p_top", [P, H + 1])
        gtop = sb("p_gtop", [P, H + 1])
        vclip = sb("p_vclip", [P, 1])
        vinv = sb("p_vinv", [P, 1])
        alpha = sb("p_alpha", [P, 1])
        dE = sb("p_dE", [P, NT, H])
        z = sb("p_z", [P, NT, H])
        z5 = sb("p_z5", [P, NT, H])
        m = sb("p_m", [P, NT, H])
        srow = sb("p_srow", [NT, H, P])
        psX = [ps(f"p_psX{k}", [P, KD, CH]) for k in range(2)]
        psP = ps("p_psP", [P, TILES, 512])

        s_w = sem("p_w_loaded")
        s_a = sem("p_a_loaded")
        s_id = sem("p_identity")
        s_const = sem("p_const")
        s_fold = sem("p_fold")
        s_carry = sem("p_wait_carrier")
        s_x = [sem(f"p_x_loaded{k}") for k in range(RING)]
        s_stats = sem("p_stats_ready")
        s_aggr = sem("p_aggr_ready")
        s_std = sem("p_std_ready")
        s_rstd = sem("p_rstd_ready")
        s_xn = sem("p_xn_ready")
        s_xps = sem("p_xT_in_psum")
        s_xT = sem("p_xT_ready")
        s_pp = sem("p_proj_in_psum")
        s_xto = sem("p_xt_ready")
        s_sd = sem("p_srcdst_ready")
        s_xtst = [sem("p_xt_stored0"), sem("p_xt_stored1")]
        s_vp = sem("p_vpart_ready")
        s_top = sem("p_top_ready")
        s_gtop = sem("p_gtop_ready")
        s_f = sem("p_factor_steps")
        s_act = sem("p_factor_exps")
        s_st = sem("p_srcT_in_psum")
        s_srow = sem("p_srow_ready")
        s_sst = sem("p_src_stored")

        xt_v = xt_dram.rearrange("(c t p) f -> c p t f", p=P, t=TILES)
        x_v = x.rearrange("(c t p) d -> c p t d", p=P, t=TILES)
        block = ctx.enter_context(nc.Block())

        @block.gpsimd
        def _(pool):
            make_identity(nc, pool, ident, s_id)
            nc.gpsimd.memset(eps[:, :], LN_EPS).then_inc(s_const, 1)
            pool.wait_ge(s_top, H + 1)
            nc.gpsimd.partition_all_reduce(gtop[:, :], top[:, :], P, RMAX).then_inc(s_gtop, 1)

        @block.sync
        def _(sp):
            sp.dma_start(xin[0][:, :, :], x_v[0]).then_inc(s_x[0], 16)
            for k in range(KD):
                sp.dma_start(wext[:, k, 0:H * O].rearrange("p (h o) -> p h o", h=H),
                             gnn_w[:, k * P:(k + 1) * P, :].rearrange("h p o -> p h o")).then_inc(s_w, 16)
            sp.dma_start(arow[:, :, :, :].rearrange("p h s o -> p (h s o)"),
                         gnn_a.rearrange("(u h) f -> u (h f)", u=1).broadcast_to([P, H * 2 * O])
                         ).then_inc(s_a, 16)
            for c in range(1, RING):
                sp.dma_start(xin[c][:, :, :], x_v[c]).then_inc(s_x[c], 16)
            with sp.Fori(0, NC // RING - 1) as i:
                for slot in range(RING):
                    sp.wait_ge(s_xn, RING * i + slot + 1)
                    sp.dma_start(xin[slot][:, :, :], x_v[RING * (i + 1) + slot]).then_inc(s_x[slot], 16)
            sp.wait_ge(s_srow, 1)
            sp.dma_start(s_dram.rearrange("h (t p) -> t h p", p=P), srow[:, :, :]).then_inc(s_sst, 16)
            sp.wait_ge(s_sst, 16)

        @block.vector
        def _(dve):
            def fold():
                dve.wait_ge(s_w, 16 * KD)
                dve.wait_ge(s_a, 16)
                for k in range(KD):
                    w3 = wext[:, k, 0:H * O].rearrange("p (h o) -> p h o", h=H)
                    if k:
                        dve.wait_ge(s_fold, 3 * k)
                    for half in range(2):
                        nc.vector.tensor_tensor(wprod[:, :, half, :], w3, arow[:, :, half, :],
                                                ALU.mult).then_inc(s_fold, 1)
                    dve.wait_ge(s_fold, 3 * k + 2)
                    nc.vector.tensor_reduce(wext[:, k, H * O:W1].rearrange("p (s h) -> p h s", s=2),
                                            wprod[:, :, :, :], AX, ALU.add).then_inc(s_fold, 1)

            def measure(c, slot, turn):
                dve.wait_ge(s_x[slot], 16 * turn + 16)
                for t in range(TILES):
                    last = nc.vector.bn_stats(stats[slot % 2][:, t, :], xin[slot][:, t, :])
                last.then_inc(s_stats, 1)
                dve.wait_ge(s_stats, c + 1)
                if past(c, 2):
                    dve.wait_ge(s_std, c - 1)
                dve.sem_inc(s_carry, 1)
                for t in range(TILES):
                    last = nc.vector.bn_aggr(meanvar[slot % 2][:, t, :], stats[slot % 2][:, t, :])
                last.then_inc(s_aggr, 1)

            def normalise(c, slot):
                k = slot % 2
                dve.wait_ge(s_std, c + 1)
                nc.vector.reciprocal(rstd[k][:, :], std[k][:, :]).then_inc(s_rstd, 1)
                dve.wait_ge(s_rstd, c + 1)
                if past(c, 2):
                    dve.wait_ge(s_xps, c - 1)
                for t in range(TILES):
                    last = nc.vector.tensor_scalar(xn[k][:, t, :], xin[slot][:, t, :],
                                                   meanvar[k][:, t, 0:1], rstd[k][:, t:t + 1],
                                                   ALU.subtract, ALU.mult)
                last.then_inc(s_xn, 1)

            def keep_scores(c, slot):
                k = slot % 2
                dve.wait_ge(s_xto, c + 1)
                nc.vector.tensor_reduce(vpart[:, bass.ds(c, 1)], xto[k][:, :, 0:H * O], mybir.AxisListType.XY,
                                        ALU.max, apply_absolute_value=True).then_inc(s_vp, 1)
                nc.vector.tensor_copy(srcdst[:, bass.ds(c * TILES, TILES), :],
                                      xto[k][:, :, H * O:W1]).then_inc(s_sd, 1)

            def step(i, slot):
                c = RING * i + slot
                measure(c, slot, i)
                if past(c, 1):
                    normalise(c - 1, (slot - 1) % RING)
                if isinstance(c, int) and c == 1:
                    fold()
                if past(c, 3):
                    keep_scores(c - 3, (slot - 3) % RING)

            turns(dve, NC, RING, step)
            normalise(NC - 1, RING - 1)
            for c in range(NC - 3, NC):
                keep_scores(c, c % RING)
            dve.wait_ge(s_sd, NC)
            dve.wait_ge(s_vp, NC)
            src = srcdst[:, :, 0:H]
            dst = srcdst[:, :, H:2 * H]
            for h in range(H):
                nc.vector.tensor_reduce(top[:, h:h + 1], srcdst[:, :, H + h], AX, ALU.max).then_inc(s_top, 1)
            nc.vector.tensor_reduce(top[:, H:H + 1], vpart[:, :], AX, ALU.max).then_inc(s_top, 1)
            dve.wait_ge(s_st, 1)
            nc.vector.tensor_copy(srow[:, :, :], psX[0][0:NT, 0, :].rearrange("p (h i) -> p h i", h=H)).then_inc(s_srow, 1)
            dve.wait_ge(s_gtop, 1)
            D_b = gtop[:, 0:H].unsqueeze(1).broadcast_to([P, NT, H])
            nc.vector.tensor_tensor(dE[:, :, :], dst, D_b, ALU.subtract).then_inc(s_f, 1)
            nc.vector.tensor_tensor(z[:, :, :], src, D_b, ALU.add).then_inc(s_f, 1)
            nc.vector.tensor_scalar(vclip[:, :], gtop[:, H:H + 1], 1.0, None, ALU.max).then_inc(s_f, 1)
            nc.vector.tensor_scalar(dsharp[:, :, :], dst, SHARP, None, ALU.mult).then_inc(s_f, 1)
            nc.vector.tensor_scalar(ndst[:, :], dst[:, :, H - 1], -1.0, None, ALU.mult)
            dve.wait_ge(s_f, 4)
            nc.vector.reciprocal(vinv[:, :], vclip[:, :]).then_inc(s_f, 1)
            nc.vector.tensor_scalar(z5[:, :, :], z[:, :, :], SLOPE, None, ALU.mult).then_inc(s_f, 1)
            dve.wait_ge(s_f, 6)
            nc.vector.tensor_scalar(alpha[:, :], vinv[:, :], HALF_TOP, None, ALU.mult).then_inc(s_f, 1)
            nc.vector.tensor_tensor(m[:, :, :], z[:, :, :], z5[:, :, :], ALU.max).then_inc(s_f, 1)
            dve.wait_ge(s_f, 8)
            nc.vector.tensor_tensor(z[:, :, :], z[:, :, :], m[:, :, :], ALU.subtract).then_inc(s_f, 1)
            nc.vector.tensor_tensor(z5[:, :, :], z5[:, :, :], m[:, :, :], ALU.subtract).then_inc(s_f, 1)
            dve.wait_ge(s_act, 2)
            nc.vector.tensor_scalar(E[:, :, :], E[:, :, :], alpha[:, 0:1], None, ALU.mult).then_inc(s_f, 1)
            nc.vector.tensor_scalar(F[:, :, :], F[:, :, :], alpha[:, 0:1], None, ALU.mult).then_inc(s_f, 1)

        @block.scalar
        def _(act):
            act.wait_ge(s_const, 1)

            def root(c, slot):
                act.wait_ge(s_aggr, c + 1)
                if past(c, 2):
                    act.wait_ge(s_rstd, c - 1)
                nc.scalar.activation(std[slot % 2][:, :], meanvar[slot % 2][:, :, 1], ACT.Sqrt,
                                     bias=eps[:, 0:1]).then_inc(s_std, 1)

            def turned(c, slot):
                act.wait_ge(s_xps, c + 1)
                nc.scalar.activation(xnT[slot % 2][:, :, :], psX[slot % 2][:, :, :], ACT.Copy).then_inc(s_xT, 1)

            def projected(c, slot, turn2):
                k = slot % 2
                act.wait_ge(s_pp, c + 1)
                if past(c, 2):
                    act.wait_ge(s_xtst[k], 16 * turn2)
                    act.wait_ge(s_sd, c - 1)
                nc.scalar.activation(xto[k][:, :, :], psP[:, :, 0:W1], ACT.Copy).then_inc(s_xto, 1)
                act.wait_ge(s_xto, c + 1)
                act.dma_start(xt_v[c], xto[k][:, :, 0:H * O]).then_inc(s_xtst[k], 16)

            def step(i, slot):
                c = RING * i + slot
                root(c, slot)
                if past(c, 1):
                    turned(c - 1, (slot - 1) % RING)
                if past(c, 2):
                    projected(c - 2, (slot - 2) % RING, RING // 2 * i + slot // 2 - 1)

            turns(act, NC, RING, step)
            turned(NC - 1, RING - 1)
            projected(NC - 2, RING - 2, NC // 2 - 1)
            projected(NC - 1, RING - 1, NC // 2 - 1)
            act.wait_ge(s_f, 1)
            nc.scalar.activation(E[:, :, :], dE[:, :, :], ACT.Exp).then_inc(s_act, 1)
            nc.scalar.activation(F[:, :, :], dE[:, :, :], ACT.Exp, scale=SLOPE).then_inc(s_act, 1)
            act.wait_ge(s_f, 10)
            nc.scalar.activation(cE[:, :, :], z[:, :, :], ACT.Exp).then_inc(s_act, 1)
            nc.scalar.activation(cF[:, :, :], z5[:, :, :], ACT.Exp).then_inc(s_act, 1)
            for slot in range(2):
                act.wait_ge(s_xtst[slot], 16 * (NC // 2))

        @block.tensor
        def _(pe):
            pe.wait_ge(s_id, 2)

            def turn(c, slot):
                k = slot % 2
                pe.wait_ge(s_xn, c + 1)
                if past(c, 2):
                    pe.wait_ge(s_xT, c - 1)
                for t in range(TILES):
                    for kd in range(KD):
                        last = nc.tensor.transpose(psX[k][:, kd, t * P:(t + 1) * P],
                                                   xn[k][:, t, kd * P:(kd + 1) * P], ident[:, :])
                last.then_inc(s_xps, 1)

            def products(c, slot):
                pe.wait_ge(s_xT, c + 1)
                if not past(c, 1):
                    pe.wait_ge(s_fold, 3 * KD)
                else:
                    pe.wait_ge(s_xto, c)
                for t in range(TILES):
                    for kd in range(KD):
                        last = nc.tensor.matmul(psP[:, t, 0:W1], xnT[slot % 2][:, kd, t * P:(t + 1) * P],
                                                wext[:, kd, :], start=(kd == 0), stop=(kd == KD - 1))
                last.then_inc(s_pp, 1)

            def step(i, slot):
                c = RING * i + slot
                turn(c, slot)
                if past(c, 1):
                    products(c - 1, (slot - 1) % RING)

            turns(pe, NC, RING, step)
            products(NC - 1, RING - 1)
            pe.wait_ge(s_sd, NC)
            for h in range(H):
                last = nc.tensor.transpose(psX[0][0:NT, 0, h * P:(h + 1) * P], srcdst[:, :, h], ident[:, :])
            last.then_inc(s_st, 1)


def split_rows(nc, xt_dram, V, keep, N, H, O):
    NT, NC = N // P, N // CH
    E, F = keep["E"], keep["F"]
    with ExitStack() as ctx:
        def sb(name, shape, dt=F32):
            return ctx.enter_context(nc.sbuf_tensor(name, shape, dt))

        def sem(name):
            return ctx.enter_context(nc.semaphore(name))

        RING = 4
        xt = [sb(f"v_xt{k}", [P, TILES, H, O]) for k in range(RING)]
        prod = [[sb(f"v_prod{f}_{k}", [P, TILES, H, O]) for k in range(2)] for f in "EF"]
        s_xt = [sem(f"v_xt_loaded{k}") for k in range(RING)]
        s_prod = [sem("v_prodE_ready"), sem("v_prodF_ready")]
        s_hi = [sem("v_hiE_ready"), sem("v_hiF_ready")]
        s_lo = [sem("v_loE_ready"), sem("v_loF_ready")]
        s_one = sem("v_ones_hi")
        s_onelo = sem("v_ones_lo")
        xt_v = xt_dram.rearrange("(c t p) f -> c p t f", p=P, t=TILES)
        block = ctx.enter_context(nc.Block())

        def tile_rows(c, term):
            return V[:, bass.ds(c * TILES, TILES), term, :, 0:O]

        def multiply(eng, ops, f, c, slot, turn):
            eng.wait_ge(s_xt[slot], 16 * turn + 16)
            if past(c, 2):
                eng.wait_ge(s_lo[f], c - 1)
            fb = (E, F)[f][:, bass.ds(c * TILES, TILES), :].unsqueeze(3).broadcast_to([P, TILES, H, O])
            ops.tensor_tensor(prod[f][slot % 2][:, :, :, :], xt[slot][:, :, :, :], fb,
                              ALU.mult).then_inc(s_prod[f], 1)

        @block.sync
        def _(sp):
            def load(c, slot):
                sp.dma_start(xt[slot][:, :, :, :].rearrange("p t h o -> p t (h o)"),
                             xt_v[c]).then_inc(s_xt[slot], 16)

            for c in range(RING):
                load(c, c)
            with sp.Fori(0, NC // RING - 1) as i:
                for slot in range(RING):
                    c = RING * i + slot
                    sp.wait_ge(s_prod[0], c + 1)
                    sp.wait_ge(s_prod[1], c + 1)
                    load(c + RING, slot)

        @block.gpsimd
        def _(pool):
            turns(pool, NC, RING, lambda i, slot: multiply(pool, nc.gpsimd, 1, RING * i + slot, slot, i))

        @block.scalar
        def _(act):
            for f, fac in enumerate((E, F)):
                last = nc.scalar.activation(V[:, :, 2 * f, :, O], fac[:, :, :], ACT.Copy)
            last.then_inc(s_one, 1)

            def step(i, slot):
                c = RING * i + slot
                for f in range(2):
                    act.wait_ge(s_prod[f], c + 1)
                    nc.scalar.activation(tile_rows(c, 2 * f), prod[f][slot % 2][:, :, :, :],
                                         ACT.Copy).then_inc(s_hi[f], 1)

            turns(act, NC, RING, step)

        @block.vector
        def _(dve):
            dve.wait_ge(s_one, 1)
            for f, fac in enumerate((E, F)):
                nc.vector.tensor_tensor(V[:, :, 2 * f + 1, :, O], fac[:, :, :], V[:, :, 2 * f, :, O],
                                        ALU.subtract).then_inc(s_onelo, 1)

            def low(c, slot, f):
                dve.wait_ge(s_hi[f], c + 1)
                nc.vector.tensor_tensor(tile_rows(c, 2 * f + 1), prod[f][slot % 2][:, :, :, :],
                                        tile_rows(c, 2 * f), ALU.subtract).then_inc(s_lo[f], 1)

            def step(i, slot):
                c = RING * i + slot
                multiply(dve, nc.vector, 0, c, slot, i)
                if past(c, 1):
                    for f in range(2):
                        low(c - 1, (slot - 1) % RING, f)

            turns(dve, NC, RING, step)
            for f in range(2):
                low(NC - 1, RING - 1, f)


def attend(nc, x, adj, s_dram, x1_dram, V, keep, H, O):
    N, D = x.shape
    NT, NC = N // P, N // CH
    PAIRS = NT // 2
    COLS = 4 * P
    LOADS = N // COLS
    PPL = COLS // P // 2
    O1 = O + 1
    EXPLICIT = 3
    IMPLICIT = H - EXPLICIT
    TH = TILES * H
    PER = 512 // O1
    NG = 2 * TH + TILES * IMPLICIT
    NB = -(-NG // PER)
    NBA = NB // 2
    GROUPS = ((0, 1), (2, 3))
    SHARE = 4
    DENS = 5
    STEPS = 5
    cE, cF, dsharp, ndst = (keep[name] for name in ("cE", "cF", "dsharp", "ndst"))
    with ExitStack() as ctx:
        def sb(name, shape, dt=F32):
            return ctx.enter_context(nc.sbuf_tensor(name, shape, dt))

        def sem(name):
            return ctx.enter_context(nc.semaphore(name))

        ident = sb("g_ident", [P, P], BF16)
        araw = [sb(f"g_araw{k}", [P, TILES, COLS], BF16) for k in range(2)]
        src = [sb(f"g_src{h}", [P, CH]) for h in range(H)]
        step = sb("g_step", [P, H, 2, CH], F16)
        A = [sb(f"g_A{k}", [P, 2, CH], F16) for k in range(4)]
        B = [sb(f"g_B{k}", [P, H, 2, CH], F16) for k in range(2)]
        C = [sb(f"g_C{k}", [P, EXPLICIT, 2, CH], F16) for k in range(2)]
        sums = sb("g_sums", [P, NG, O1])
        den = sb("g_den", [P, 2, TH])
        rden = sb("g_rden", [P, TH])
        weights = sb("g_weights", [P, 2, TH])
        xrow = sb("g_xrow", [P, TH, O])
        acc = ctx.enter_context(nc.psum_tensor("g_acc", [P, NB, 512], F32))
        turned = [ctx.enter_context(nc.psum_tensor(f"g_turned{k}", [P, 2, CH], BF16)) for k in range(2)]

        s_id = sem("g_identity")
        s_adj = [sem("g_adj_loaded0"), sem("g_adj_loaded1")]
        s_src = [sem(f"g_src{h}_loaded") for h in range(H)]
        s_turn = sem("g_turned_pairs")
        s_A = sem("g_A_ready")
        s_step = sem("g_step_ready")
        s_B = sem("g_B_ready")
        s_masks = sem("g_masks_ready")
        s_used = sem("g_masks_used")
        s_sumA = sem("g_sums_by_act")
        s_sumD = sem("g_sums_by_dve")
        s_den = sem("g_den_steps")
        s_post = sem("g_post_steps")
        s_x = sem("g_x_loaded")
        s_out = sem("g_x1_stored")
        s_carry = sem("g_wait_carrier")

        adj_v = adj.rearrange("(c t p) (l j) -> c l p t j", p=P, t=TILES, j=COLS)
        x_v = x.rearrange("(c t p) d -> c p t d", p=P, t=TILES)
        x1_v = x1_dram.rearrange("(c t p) d -> c p t d", p=P, t=TILES)
        xrow_v = xrow[:, :, :].rearrange("p (t h) o -> p t (h o)", t=TILES)

        def slot_of(g):
            return acc[:, g // PER, O1 * (g % PER):O1 * (g % PER) + O1]

        def compared_by_dve(p):
            return p % SHARE == SHARE // 2

        def evacuate(copy, banks, done):
            for b in banks:
                n = min(PER, NG - b * PER)
                last = copy(sums[:, b * PER:b * PER + n, :].rearrange("p g o -> p (g o)"), acc[:, b, 0:n * O1])
            last.then_inc(done, 1)

        def post(eng, tt, c, k):
            Es, Fs = sums[:, 0:TH, 0:O], sums[:, TH:2 * TH, 0:O]

            def bc(n):
                return weights[:, n, :].unsqueeze(2).broadcast_to([P, TH, O])

            if k == 0:
                eng.wait_ge(s_sumA, c + 2)
                eng.wait_ge(s_sumD, c + 2)
                f = Fs.rearrange("p (t h) o -> p t h o", t=TILES)[:, :, EXPLICIT:H, :]
                af = sums[:, 2 * TH:NG, 0:O].rearrange("p (t h) o -> p t h o", t=TILES)
                tt(f, af, f, ALU.subtract).then_inc(s_post, 1)
            elif k == 1:
                eng.wait_ge(s_den, DENS * (c + 1))
                tt(Es, Es, bc(0), ALU.mult).then_inc(s_post, 1)
            elif k == 2:
                eng.wait_ge(s_post, STEPS * (c + 1) + 1)
                tt(Fs, Fs, bc(1), ALU.mult).then_inc(s_post, 1)
            elif k == 3:
                eng.wait_ge(s_post, STEPS * (c + 1) + 3)
                tt(Es, Es, Fs, ALU.add).then_inc(s_post, 1)
            else:
                eng.wait_ge(s_post, STEPS * (c + 1) + 4)
                eng.wait_ge(s_x, 16 * c + 16)
                tt(xrow[:, :, :], xrow[:, :, :], Es, ALU.add).then_inc(s_post, 1)

        block = ctx.enter_context(nc.Block())

        @block.sync
        def _(sp):
            def load_src(c, h):
                rows = s_dram[h:h + 1, bass.ds(c * CH, CH)].broadcast_to([P, CH])
                sp.dma_start(src[h][:, :], rows).then_inc(s_src[h], 16)

            def chunk(c, last):
                sp.dma_start(xrow_v, x_v[c]).then_inc(s_x, 16)
                if not last:
                    for h in range(H):
                        sp.wait_ge(s_step, len(GROUPS) * (PAIRS * (c + 1) - 1) + h // 2 + 1)
                        load_src(c + 1, h)
                sp.wait_ge(s_post, STEPS * (c + 2))
                sp.dma_start(x1_v[c], xrow_v).then_inc(s_out, 16)
                sp.wait_ge(s_out, 16 * c + 16)
                sp.sem_inc(s_carry, 1)

            for h in range(H):
                load_src(0, h)
            with sp.Fori(0, NC - 1) as c:
                chunk(c, False)
            chunk(NC - 1, True)

        @block.gpsimd
        def _(pool):
            def load(c, l):
                pool.dma_start(araw[l % 2][:, :, :], adj_v[c, l]).then_inc(s_adj[l % 2], 16)

            def reload(c, l):
                pool.wait_ge(s_turn, PAIRS * c + PPL * (l + 1))
                if l + 2 < LOADS:
                    load(c, l + 2)
                else:
                    load(c + 1, l + 2 - LOADS)

            pool.sem_inc(s_post, STEPS)
            make_identity(nc, pool, ident, s_id)
            load(0, 0)
            load(0, 1)
            for l in range(4):
                reload(0, l)
            with pool.Fori(0, NC - 1) as c:
                for l in range(4, LOADS):
                    reload(c, l)
                for l in range(4):
                    reload(c + 1, l)
                    for k in {1: (0, 1), 2: (2, 3), 3: (4,)}.get(l, ()):
                        post(pool, nc.gpsimd.tensor_tensor, c, k)
            for l in range(4, LOADS - 2):
                reload(NC - 1, l)

        @block.scalar
        def _(act):
            def steps(c, p, g):
                q = PAIRS * c + p
                if past(q, 1):
                    act.wait_ge(s_B, len(GROUPS) * (q - 1) + g + 1)
                for h in GROUPS[g]:
                    if p == 0:
                        act.wait_ge(s_src[h], 16 * c + 16)
                    for jj in range(1 if h == H - 1 and compared_by_dve(p) else 2):
                        last = nc.scalar.activation(step[:, h, jj, :], src[h][:, :], ACT.Sigmoid,
                                                    bias=dsharp[:, 2 * p + jj, h:h + 1], scale=SHARP)
                last.then_inc(s_step, 1)

            def pair(c, p):
                steps(c, p, 0)
                steps(c, p, 1)

            def sums_out(c):
                act.wait_ge(s_used, len(GROUPS) * PAIRS * (c + 1))
                act.wait_ge(s_post, STEPS * (c + 1))
                evacuate(lambda o, i: nc.scalar.activation(o, i, ACT.Copy), range(NBA), s_sumA)

            act.sem_inc(s_sumA, 1)
            pair(0, 0)
            steps(0, 1, 0)
            with act.Fori(0, NC - 1) as c:
                steps(c, 1, 1)
                for p in range(2, PAIRS):
                    pair(c, p)
                pair(c + 1, 0)
                steps(c + 1, 1, 0)
                sums_out(c)
            steps(NC - 1, 1, 1)
            for p in range(2, PAIRS):
                pair(NC - 1, p)
            sums_out(NC - 1)

        @block.vector
        def _(dve):
            def make_A(c, p):
                q = PAIRS * c + p
                dve.wait_ge(s_turn, q + 1)
                nc.vector.tensor_scalar(A[p % 4][:, :, :], turned[p % 2][:, :, :], 0.0, None,
                                        ALU.is_gt).then_inc(s_A, 1)

            def nothing(n=0):
                pass

            def pair(c, p, next_A, between=nothing):
                q = PAIRS * c + p
                k = p % 2

                def times(heads):
                    n = len(heads)
                    return A[p % 4][:, :, :].unsqueeze(1).broadcast_to([P, n, 2, CH])

                def both(group, made):
                    shared = H - 1 in group and compared_by_dve(p)
                    if shared:
                        nc.vector.scalar_tensor_tensor(out=B[k][:, H - 1, 1, :], in0=src[H - 1][:, :],
                                                       scalar=ndst[:, 2 * p + 1:2 * p + 2],
                                                       in1=A[p % 4][:, 1, :], op0=ALU.is_gt, op1=ALU.mult)
                    dve.wait_ge(s_step, made)
                    if shared:
                        nc.vector.tensor_tensor(B[k][:, H - 1, 0, :], step[:, H - 1, 0, :], A[p % 4][:, 0, :],
                                                ALU.mult)
                        group = group[:-1]
                    at = slice(group[0], group[-1] + 1)
                    nc.vector.tensor_tensor(B[k][:, at, :, :], step[:, at, :, :], times(group),
                                            ALU.mult).then_inc(s_B, 1)

                def other(group, made):
                    group = [h for h in group if h < EXPLICIT]
                    dve.wait_ge(s_B, made)
                    at = slice(group[0], group[-1] + 1)
                    nc.vector.tensor_tensor(C[k][:, at, :, :], times(group), B[k][:, at, :, :],
                                            ALU.subtract).then_inc(s_masks, 1)

                dve.wait_ge(s_A, q + 1)
                if past(q, 2):
                    dve.wait_ge(s_used, 2 * q - 3)
                both(GROUPS[0], 2 * q + 1)
                between(0)
                next_A()
                between(1)
                if past(q, 2):
                    dve.wait_ge(s_used, 2 * q - 2)
                both(GROUPS[1], 2 * q + 2)
                between(2)
                other(GROUPS[0], 2 * q + 1)
                between(3)
                other(GROUPS[1], 2 * q + 2)
                between(4)

            def sums_out(c):
                dve.wait_ge(s_used, len(GROUPS) * PAIRS * (c + 1))
                dve.wait_ge(s_post, STEPS * (c + 1))
                evacuate(lambda o, i: nc.vector.tensor_copy(o, i), range(NBA, NB), s_sumD)

            def denominators(c, n):
                at = bass.ds(c * TILES, TILES)
                four = "p (t h) -> p t h"
                Ed, Fd = sums[:, 0:TH, O], sums[:, TH:2 * TH, O]
                fd = Fd.rearrange(four, t=TILES)[:, :, EXPLICIT:H]
                af = sums[:, 2 * TH:NG, O].rearrange(four, t=TILES)
                if n == 0:
                    dve.wait_ge(s_sumD, c + 2)
                    dve.wait_ge(s_sumA, c + 2)
                    nc.vector.tensor_tensor(fd, af, fd, ALU.subtract)
                    nc.vector.tensor_tensor(den[:, 0, :].rearrange(four, t=TILES), Ed.rearrange(four, t=TILES),
                                            cE[:, at, :], ALU.mult).then_inc(s_den, 1)
                elif n == 1:
                    dve.wait_ge(s_den, DENS * c + 1)
                    nc.vector.tensor_tensor(den[:, 1, :].rearrange(four, t=TILES), Fd.rearrange(four, t=TILES),
                                            cF[:, at, :], ALU.mult).then_inc(s_den, 1)
                elif n == 2:
                    dve.wait_ge(s_den, DENS * c + 2)
                    nc.vector.tensor_tensor(den[:, 0, :], den[:, 0, :], den[:, 1, :], ALU.add).then_inc(s_den, 1)
                elif n == 3:
                    dve.wait_ge(s_den, DENS * c + 3)
                    nc.vector.reciprocal(rden[:, :], den[:, 0, :]).then_inc(s_den, 1)
                else:
                    dve.wait_ge(s_den, DENS * c + 4)
                    for k, fac in enumerate((cE, cF)):
                        last = nc.vector.tensor_tensor(weights[:, k, :].rearrange(four, t=TILES), fac[:, at, :],
                                                       rden[:, :].rearrange(four, t=TILES), ALU.mult)
                    last.then_inc(s_den, 1)

            dve.sem_inc(s_sumD, 1)
            def A_after(c, p):
                return lambda: make_A(c, p + 1) if p + 1 < PAIRS else make_A(c + 1, 0)

            make_A(0, 0)
            for p in range(2):
                pair(0, p, A_after(0, p))
            with dve.Fori(0, NC - 1) as c:
                for p in range(2, PAIRS):
                    pair(c, p, A_after(c, p))
                pair(c + 1, 0, A_after(c + 1, 0))
                sums_out(c)
                pair(c + 1, 1, A_after(c + 1, 1), lambda n: denominators(c, n))
            for p in range(2, PAIRS):
                pair(NC - 1, p, A_after(NC - 1, p) if p + 1 < PAIRS else nothing)
            sums_out(NC - 1)
            for n in range(DENS):
                denominators(NC - 1, n)
            for k in range(STEPS):
                post(dve, nc.vector.tensor_tensor, NC - 1, k)

        @block.tensor
        def _(pe):
            def turn(c, p):
                k = p % 2
                if p % PPL == 0:
                    l = p // PPL
                    pe.wait_ge(s_adj[l % 2], 16 * (LOADS // 2 * c + l // 2 + 1))
                if p == 2:
                    pe.wait_ge(s_A, PAIRS * c + 1)
                for jj in range(2):
                    col = (2 * (p % PPL) + jj) * P
                    for t in range(TILES):
                        last = nc.tensor.transpose(turned[k][:, jj, t * P:(t + 1) * P],
                                                   araw[p // PPL % 2][:, t, col:col + P], ident[:, :])
                last.then_inc(s_turn, 1)

            def products(c, p, open_banks):
                k = p % 2
                for n, group in enumerate(GROUPS):
                    pe.wait_ge(s_masks, len(GROUPS) * (PAIRS * c + p) + n + 1)
                    if p == 0 and n == 0:
                        pe.wait_ge(s_sumA, c + 1)
                        pe.wait_ge(s_sumD, c + 1)
                    for jj in range(2):
                        for t in range(TILES):
                            last = group_products(group, k, A[p % 4], jj, t, 2 * p + jj, open_banks)
                    last.then_inc(s_used, 1)

            def group_products(group, k, a, jj, t, jb, open_banks):
                def add(mask, term, h, g):
                    for part in range(2):
                        opens = jb == 0 and part == 0 and g // PER not in open_banks
                        x = nc.tensor.matmul(slot_of(g), mask[:, t * P:(t + 1) * P],
                                             V[:, jb, 2 * term + part, h, :], start=opens,
                                             stop=(jb == NT - 1 and part == 1), skip_group_check=True)
                        if opens:
                            open_banks.add(g // PER)
                    return x

                for h in group:
                    g = t * H + h
                    add(B[k][:, h, jj, :], 0, h, g)
                    if h < EXPLICIT:
                        last = add(C[k][:, h, jj, :], 1, h, TH + g)
                    else:
                        add(B[k][:, h, jj, :], 1, h, TH + g)
                        last = add(a[:, jj, :], 1, h, 2 * TH + t * IMPLICIT + h - EXPLICIT)
                return last

            pe.wait_ge(s_id, 2)
            turn(0, 0)
            turn(0, 1)
            with pe.Fori(0, NC - 1) as c:
                open_banks = set()
                for p in range(PAIRS):
                    turn(c, p + 2) if p + 2 < PAIRS else turn(c + 1, p + 2 - PAIRS)
                    products(c, p, open_banks)
            open_banks = set()
            for p in range(PAIRS):
                if p + 2 < PAIRS:
                    turn(NC - 1, p + 2)
                products(NC - 1, p, open_banks)


def mixture(nc, x1_dram, gamma, beta, wr, br, w1, b1, w2, b2, out):
    N, D = x1_dram.shape
    NE, _, HID = w1.shape
    DO = w2.shape[2]
    NC, KD, M = N // CH, D // P, HID // P
    NT_C = NE * M
    RING = 4
    AHEAD = 2
    STRIP = 32
    WRING = 4
    ROWS = NE * M + 2 * KD
    with ExitStack() as ctx:
        def sb(name, shape, dt=F32):
            return ctx.enter_context(nc.sbuf_tensor(name, shape, dt))

        def sem(name):
            return ctx.enter_context(nc.semaphore(name))

        w1h = sb("f_w1h", [P, NE, KD, HID], F32R)
        w1l = sb("f_w1l", [P, NE, KD, HID], F32R)
        w2h = sb("f_w2h", [P, NE, M, DO], F32R)
        w2l = sb("f_w2l", [P, NE, M, DO], F32R)
        wraw = [sb(f"f_wraw{k}", [P, KD * HID]) for k in range(WRING)]
        ident = sb("f_ident", [P, P])
        rows = sb("f_rows", [ROWS, P])
        cols = sb("f_cols", [P, ROWS])
        wrs = sb("f_wr", [P, KD, NE])
        brow = sb("f_br", [P, NE])
        b2r = sb("f_b2r", [3 * STRIP, DO], F32R)
        gsplit = sb("f_gsplit", [P, TILES, 3 * STRIP], F32R)
        iota = sb("f_iota", [P, NE])
        eps = sb("f_eps", [P, 1])
        xs = [sb(f"f_xs{k}", [P, TILES, D]) for k in range(2)]
        nrm = sb("f_nrm", [P, TILES, D])
        stats = sb("f_stats", [P, TILES, 6])
        meanvar = sb("f_meanvar", [P, TILES, 2])
        std = sb("f_std", [P, TILES])
        rstd = sb("f_rstd", [P, TILES])
        xT = sb("f_xT", [P, KD, CH])
        xTh = [sb(f"f_xTh{k}", [P, KD, CH], F32R) for k in range(2)]
        xTl = [sb(f"f_xTl{k}", [P, KD, CH], F32R) for k in range(2)]
        logits = sb("f_logits", [P, TILES, NE])
        best = sb("f_best", [P, TILES, 8])
        where = sb("f_where", [P, TILES, 8], U32)
        wheref = sb("f_wheref", [P, TILES, 2])
        gap = sb("f_gap", [P, TILES])
        egap = sb("f_egap", [P, TILES])
        onep = sb("f_onep", [P, TILES])
        wtop = sb("f_wtop", [P, 2, TILES])
        pick = sb("f_pick", [P, 2, TILES, NE])
        gates = [sb(f"f_gates{k}", [P, TILES, NE]) for k in range(2)]
        gatesT = sb("f_gatesT", [3 * STRIP, CH], F32R)
        hid = [sb(f"f_hid{k}", [P, CH]) for k in range(RING)]
        hidh = [sb(f"f_hidh{k}", [P, CH], F32R) for k in range(RING)]
        hidl = [sb(f"f_hidl{k}", [P, CH], F32R) for k in range(RING)]
        b2s = hid[RING - 1][0:3 * STRIP, 0:DO]
        psH = [ctx.enter_context(nc.psum_tensor(f"f_psH{k}", [P, CH], F32)) for k in range(AHEAD)]
        psY = [ctx.enter_context(nc.psum_tensor(f"f_psY{k}", [P, TILES, DO], F32)) for k in range(2)]
        psM = ctx.enter_context(nc.psum_tensor("f_psM", [P, CH], F32))

        s_row = sem("f_rows_loaded")
        s_small = sem("f_small_loaded")
        s_wload = [sem(f"f_weights_loaded{k}") for k in range(WRING)]
        s_whi = sem("f_weights_hi")
        s_wlo = sem("f_weights_lo")
        s_id = sem("f_identity")
        s_const = sem("f_const")
        s_colps = sem("f_cols_in_psum")
        s_cols = sem("f_cols_ready")
        s_x = [sem("f_x1_loaded0"), sem("f_x1_loaded1")]
        s_st = [sem("f_out_stored0"), sem("f_out_stored1")]
        s_stats1 = sem("f_stats1")
        s_aggr1 = sem("f_aggr1")
        s_std1 = sem("f_std1")
        s_rstd1 = sem("f_rstd1")
        s_nrm1 = sem("f_norm1")
        s_stats2 = sem("f_stats2")
        s_aggr2 = sem("f_aggr2")
        s_std2 = sem("f_std2")
        s_rstd2 = sem("f_rstd2")
        s_nrm2 = sem("f_norm2")
        s_tps = sem("f_xT_in_psum")
        s_xT = sem("f_xT_ready")
        s_xh = sem("f_xT_hi_ready")
        s_xl = sem("f_xT_lo_ready")
        s_lgps = sem("f_logits_in_psum")
        s_lg = sem("f_logits_ready")
        s_best = sem("f_best_ready")
        s_where = sem("f_where_ready")
        s_gap = sem("f_gap_ready")
        s_egap = sem("f_exp_gap_ready")
        s_g = sem("f_gate_steps")
        s_gates = sem("f_gates_ready")
        s_ghi = sem("f_gates_hi")
        s_glo = sem("f_gates_lo")
        s_b2r = sem("f_b2_split_steps")
        s_gtps = sem("f_gatesT_in_psum")
        s_gt = sem("f_gatesT_ready")
        s_b2ps = sem("f_b2_in_psum")
        s_b2 = sem("f_b2_added")
        s_h = sem("f_hidden_in_psum")
        s_gelu = sem("f_gelu_ready")
        s_hh = sem("f_hidden_hi")
        s_hl = sem("f_hidden_lo")
        s_y = sem("f_expert_in_psum")
        s_acc = sem("f_expert_added")
        s_carry = sem("f_wait_carrier")

        x1_v = x1_dram.rearrange("(c t p) d -> c p t d", p=P, t=TILES)
        out_v = out.rearrange("(c t p) d -> c p t d", p=P, t=TILES)
        block = ctx.enter_context(nc.Block())

        def flat(w, e):
            return w[:, e, :, :].rearrange("p k n -> p (k n)")

        def loop(eng, body):
            with eng.Fori(0, NC // 2 - 1) as i:
                for slot in range(2):
                    body(i, slot, False)
            body(NC // 2 - 1, 0, False)
            body(NC // 2 - 1, 1, True)

        @block.sync
        def _(sp):
            sp.dma_start(xs[0][:, :, :], x1_v[0]).then_inc(s_x[0], 16)
            sp.dma_start(rows[0:NE * M, :], b1.rearrange("e (m p) -> (e m) p", p=P)).then_inc(s_row, 16)
            sp.dma_start(rows[NE * M:NE * M + KD, :], gamma.rearrange("(k p) -> k p", p=P)).then_inc(s_row, 16)
            sp.dma_start(rows[NE * M + KD:ROWS, :], beta.rearrange("(k p) -> k p", p=P)).then_inc(s_row, 16)
            sp.dma_start(wrs[:, :, :], wr.rearrange("(k p) e -> p k e", p=P)).then_inc(s_small, 16)
            sp.dma_start(brow[:, :], br.rearrange("(u e) -> u e", u=1).broadcast_to([P, NE])).then_inc(s_small, 16)
            for u in range(2 * NE):
                e, k = u // 2, u % 2
                if u >= WRING:
                    sp.wait_ge(s_wlo, u - WRING + 1)
                sp.dma_start(wraw[u % WRING].rearrange("p (k n) -> p k n", k=(KD, M)[k]),
                             (w1, w2)[k][e].rearrange("(k p) n -> p k n", p=P)).then_inc(s_wload[u % WRING], 16)
                if u == 1:
                    sp.wait_ge(s_const, 3)
                    for k in range(3):
                        sp.dma_start(b2s[STRIP * k:STRIP * k + NE, :], b2).then_inc(s_small, 16)
                    sp.dma_start(xs[1][:, :, :], x1_v[1]).then_inc(s_x[1], 16)

            def store(c, slot):
                sp.wait_ge(s_acc, NE * c + NE)
                sp.dma_start(out_v[c], xs[slot][:, :, :]).then_inc(s_st[slot], 16)

            with sp.Fori(0, NC // 2 - 1) as i:
                for slot in range(2):
                    store(2 * i + slot, slot)
                    sp.wait_ge(s_st[slot], 16 * i + 16)
                    sp.dma_start(xs[slot][:, :, :], x1_v[2 * i + slot + 2]).then_inc(s_x[slot], 16)
            store(NC - 2, 0)
            store(NC - 1, 1)
            for slot in range(2):
                sp.wait_ge(s_st[slot], 16 * (NC // 2))

        @block.gpsimd
        def _(pool):
            make_identity(nc, pool, ident, s_id)
            nc.gpsimd.memset(eps[:, :], LN_EPS).then_inc(s_const, 1)
            nc.gpsimd.iota(iota[:, :], pattern=[[1, NE]], base=0, channel_multiplier=0,
                           allow_small_or_imprecise_dtypes=True).then_inc(s_const, 1)
            nc.gpsimd.memset(b2s[:, :], 0.0).then_inc(s_const, 1)
            nc.gpsimd.memset(gsplit[:, :, :].bitcast(F32), 0.0).then_inc(s_const, 1)
            for u in range(2 * NE):
                if u >= NE:
                    pool.wait_ge(s_wload[u % WRING], 16 * (u // WRING) + 16)
                    nc.gpsimd.tensor_copy(flat((w1h, w2h)[u % 2], u // 2), wraw[u % WRING][:, :]).then_inc(s_whi, 1)
                pool.wait_ge(s_whi, u + 1)
                nc.gpsimd.tensor_tensor(flat((w1l, w2l)[u % 2], u // 2), wraw[u % WRING][:, :],
                                        flat((w1h, w2h)[u % 2], u // 2).bitcast(F32),
                                        ALU.subtract).then_inc(s_wlo, 1)

        @block.scalar
        def _(act):
            def root(c, slot, aggr, done):
                act.wait_ge(aggr, c + 1)
                nc.scalar.activation(std[:, :], meanvar[:, :, 1], ACT.Sqrt, bias=eps[:, 0:1]).then_inc(done, 1)

            def turned(c, slot, k):
                g = NE * M + k
                act.wait_ge(s_tps, KD * c + k + 1)
                nc.scalar.activation(xT[:, k, :], psM[:, :], ACT.Identity, bias=cols[:, g + KD:g + KD + 1],
                                     scale=cols[:, g:g + 1]).then_inc(s_xT, 1)

            def exp_gap(c, slot):
                act.wait_ge(s_gap, c + 1)
                nc.scalar.activation(egap[:, :], gap[:, :], ACT.Exp).then_inc(s_egap, 1)

            def gates_turned(c, slot):
                act.wait_ge(s_gtps, c + 1)
                nc.scalar.activation(gatesT[:, :], psM[0:3 * STRIP, :], ACT.Copy).then_inc(s_gt, 1)

            def prepare(n, i, slot):
                c = 2 * i + slot
                if n == 8:
                    root(c, slot, s_aggr1, s_std1)
                elif n == 11:
                    root(c, slot, s_aggr2, s_std2)
                elif n == 16:
                    turned(c, slot, 0)
                elif n == 18:
                    turned(c, slot, 1)
                elif n == 22:
                    exp_gap(c, slot)
                elif n == 26:
                    gates_turned(c, slot)

            def body(i, slot, last):
                c = 2 * i + slot
                for n in range(NT_C):
                    act.wait_ge(s_h, NT_C * c + n + 1)
                    nc.scalar.activation(hid[n % RING][:, :], psH[n % AHEAD][:, :], ACT.Gelu,
                                         bias=cols[:, n:n + 1]).then_inc(s_gelu, 1)
                    if not last:
                        prepare(n, i + slot, 1 - slot)

            def high(u):
                act.wait_ge(s_wload[u % WRING], 16 * (u // WRING) + 16)
                nc.scalar.activation(flat((w1h, w2h)[u % 2], u // 2), wraw[u % WRING][:, :],
                                     ACT.Copy).then_inc(s_whi, 1)

            act.wait_ge(s_const, 2)
            act.wait_ge(s_cols, 1)
            before = {10: (0, 1), 15: (2, 3), 17: (4,), 21: (5, 6), 25: (7,)}
            for n in range(NT_C):
                for u in before.get(n, ()):
                    high(u)
                prepare(n, 0, 0)
            loop(act, body)

        @block.vector
        def _(dve):
            tt, ts = nc.vector.tensor_tensor, nc.vector.tensor_scalar

            def norm(c, src, dst, stats_done, aggr_done, std_done, rstd_done, norm_done, part):
                if part == 0:
                    for t in range(TILES):
                        last = nc.vector.bn_stats(stats[:, t, :], src[:, t, :])
                    last.then_inc(stats_done, 1)
                    dve.wait_ge(stats_done, c + 1)
                    dve.sem_inc(s_carry, 1)
                    for t in range(TILES):
                        last = nc.vector.bn_aggr(meanvar[:, t, :], stats[:, t, :])
                    last.then_inc(aggr_done, 1)
                else:
                    dve.wait_ge(std_done, c + 1)
                    nc.vector.reciprocal(rstd[:, :], std[:, :]).then_inc(rstd_done, 1)
                    dve.wait_ge(rstd_done, c + 1)
                    for t in range(TILES):
                        last = ts(dst[:, t, :], src[:, t, :], meanvar[:, t, 0:1], rstd[:, t:t + 1],
                                  ALU.subtract, ALU.mult)
                    last.then_inc(norm_done, 1)

            def norm1(c, slot, part):
                norm(c, xs[slot], nrm, s_stats1, s_aggr1, s_std1, s_rstd1, s_nrm1, part)

            def norm2(c, slot, part):
                norm(c, nrm, nrm, s_stats2, s_aggr2, s_std2, s_rstd2, s_nrm2, part)

            def split_xT(c, slot):
                dve.wait_ge(s_xT, KD * (c + 1))
                nc.vector.tensor_copy(xTh[slot][:, :, :], xT[:, :, :]).then_inc(s_xh, 1)
                dve.wait_ge(s_xh, c + 1)
                tt(xTl[slot][:, :, :], xT[:, :, :], xTh[slot][:, :, :].bitcast(F32), ALU.subtract).then_inc(s_xl, 1)

            def top2(c, slot):
                dve.wait_ge(s_lgps, c + 1)
                tt(logits[:, :, :], psM[:, 0:TILES * NE].rearrange("p (t e) -> p t e", t=TILES),
                   brow[:, :].unsqueeze(1).broadcast_to([P, TILES, NE]), ALU.add).then_inc(s_lg, 1)
                dve.wait_ge(s_lg, c + 1)
                dve.sem_inc(s_carry, 1)
                for t in range(TILES):
                    last = nc.vector.max(best[:, t, :], logits[:, t, :])
                last.then_inc(s_best, 1)
                dve.wait_ge(s_best, c + 1)
                dve.sem_inc(s_carry, 1)
                for t in range(TILES):
                    last = nc.vector.max_index(where[:, t, :], best[:, t, :], logits[:, t, :])
                last.then_inc(s_where, 1)
                tt(gap[:, :], best[:, :, 1], best[:, :, 0], ALU.subtract).then_inc(s_gap, 1)

            def make_gates(c, slot):
                dve.wait_ge(s_where, c + 1)
                nc.vector.tensor_copy(wheref[:, :, :], where[:, :, 0:2]).then_inc(s_g, 1)
                dve.wait_ge(s_egap, c + 1)
                ts(onep[:, :], egap[:, :], 1.0, None, ALU.add).then_inc(s_g, 1)
                dve.wait_ge(s_g, 6 * c + 2)
                nc.vector.reciprocal(wtop[:, 0, :], onep[:, :]).then_inc(s_g, 1)
                dve.wait_ge(s_g, 6 * c + 3)
                tt(wtop[:, 1, :], egap[:, :], wtop[:, 0, :], ALU.mult).then_inc(s_g, 1)
                dve.wait_ge(s_g, 6 * c + 4)
                for k in range(2):
                    for t in range(TILES):
                        last = ts(pick[:, k, t, :], iota[:, :], wheref[:, t, k:k + 1], wtop[:, k, t:t + 1],
                                  ALU.is_equal, ALU.mult)
                    last.then_inc(s_g, 1)
                dve.wait_ge(s_g, 6 * c + 6)
                tt(gates[slot][:, :, :], pick[:, 0, :, :], pick[:, 1, :, :], ALU.add).then_inc(s_gates, 1)
                dve.wait_ge(s_gates, c + 1)
                for k in (0, 2):
                    last = nc.vector.tensor_copy(gsplit[:, :, STRIP * k:STRIP * k + NE], gates[slot][:, :, :])
                last.then_inc(s_ghi, 1)
                dve.wait_ge(s_ghi, c + 1)
                tt(gsplit[:, :, STRIP:STRIP + NE], gates[slot][:, :, :], gsplit[:, :, 0:NE].bitcast(F32),
                   ALU.subtract).then_inc(s_glo, 1)

            def add_b2(c, slot, half):
                dve.wait_ge(s_b2ps, 2 * c + half + 1)
                two = xs[slot][:, 2 * half:2 * half + 2, :]
                tt(two, two, psM[:, :].rearrange("p (t d) -> p t d", t=2), ALU.add).then_inc(s_b2, 1)

            def prepare(n, i, slot):
                c = 2 * i + slot
                if n == 7:
                    dve.wait_ge(s_x[slot], 16 * i + 16)
                    norm1(c, slot, 0)
                elif n == 9:
                    norm1(c, slot, 1)
                    dve.wait_ge(s_nrm1, c + 1)
                    norm2(c, slot, 0)
                elif n == 12:
                    norm2(c, slot, 1)
                elif n == 19:
                    split_xT(c, slot)
                elif n == 21:
                    top2(c, slot)
                elif n == 23:
                    make_gates(c, slot)
                elif n == 28:
                    add_b2(c, slot, 0)
                elif n == 30:
                    add_b2(c, slot, 1)

            def split(c, n):
                g = NT_C * c + n
                k = n % RING
                dve.wait_ge(s_gelu, g + 1)
                nc.vector.tensor_copy(hidh[k][:, :], hid[k][:, :]).then_inc(s_hh, 1)
                dve.wait_ge(s_hh, g + 1)
                tt(hidl[k][:, :], hid[k][:, :], hidh[k][:, :].bitcast(F32), ALU.subtract).then_inc(s_hl, 1)

            def accumulate(c, slot, e):
                dve.wait_ge(s_y, NE * c + e + 1)
                if e:
                    dve.wait_ge(s_acc, NE * c + e)
                else:
                    dve.wait_ge(s_b2, 2 * c + 2)
                for t in range(TILES):
                    last = nc.vector.scalar_tensor_tensor(out=xs[slot][:, t, :], in0=psY[e % 2][:, t, :],
                                                          scalar=gates[slot][:, t, e:e + 1],
                                                          in1=xs[slot][:, t, :], op0=ALU.mult, op1=ALU.add)
                last.then_inc(s_acc, 1)

            def body(i, slot, last):
                c = 2 * i + slot
                for n in range(3, NT_C):
                    split(c, n)
                    if n % M == 2:
                        accumulate(c, slot, n // M - 1)
                    if not last:
                        prepare(n, i + slot, 1 - slot)
                if not last:
                    for n in range(3):
                        split(c + 1, n)
                accumulate(c, slot, NE - 1)

            dve.wait_ge(s_colps, 1)
            nc.vector.tensor_copy(cols[:, :], psM[:, 0:ROWS]).then_inc(s_cols, 1)
            for n in range(NT_C):
                if n == 14:
                    dve.wait_ge(s_small, 80)
                    dve.wait_ge(s_const, 4)
                    nc.vector.tensor_copy(b2r[:, :], b2s[:, :]).then_inc(s_b2r, 1)
                    dve.wait_ge(s_b2r, 1)
                    lows = slice(2 * STRIP, 3 * STRIP)
                    tt(b2r[lows, :], b2s[lows, :], b2r[lows, :].bitcast(F32), ALU.subtract).then_inc(s_b2r, 1)
                prepare(n, 0, 0)
            for n in range(3):
                split(0, n)
            loop(dve, body)

        @block.tensor
        def _(pe):
            def turn(c, slot, k):
                pe.wait_ge(s_nrm2, c + 1)
                if k:
                    pe.wait_ge(s_xT, KD * c + k)
                for t in range(TILES):
                    last = nc.tensor.transpose(psM[:, t * P:(t + 1) * P], nrm[:, t, k * P:(k + 1) * P], ident[:, :])
                last.then_inc(s_tps, 1)

            def route(c, slot):
                pe.wait_ge(s_xT, KD * (c + 1))
                for t in range(TILES):
                    for k in range(KD):
                        last = nc.tensor.matmul(psM[:, t * NE:(t + 1) * NE], xT[:, k, t * P:(t + 1) * P],
                                                wrs[:, k, :], start=(k == 0), stop=(k == KD - 1))
                last.then_inc(s_lgps, 1)

            def turn_gates(c, slot):
                pe.wait_ge(s_glo, c + 1)
                for t in range(TILES):
                    last = nc.tensor.transpose(psM[0:3 * STRIP, t * P:(t + 1) * P], gsplit[:, t, :].bitcast(F32),
                                               ident[:, :])
                last.then_inc(s_gtps, 1)

            def bias2(c, slot, half):
                pe.wait_ge(s_gt, c + 1)
                if half:
                    pe.wait_ge(s_b2, 2 * c + 1)
                for t in range(2):
                    at = (2 * half + t) * P
                    last = nc.tensor.matmul(psM[:, t * DO:(t + 1) * DO], gatesT[:, at:at + P], b2r[:, :],
                                            start=True, stop=True)
                last.then_inc(s_b2ps, 1)

            def prepare(n, i, slot):
                c = 2 * i + slot
                if n == 15:
                    turn(c, slot, 0)
                elif n == 17:
                    turn(c, slot, 1)
                elif n == 19:
                    route(c, slot)
                elif n == 25:
                    turn_gates(c, slot)
                elif n == 27:
                    bias2(c, slot, 0)
                elif n == 29:
                    bias2(c, slot, 1)

            def hidden(c, slot, n):
                e, m = n // M, n % M
                if m == 0:
                    pe.wait_ge(s_wlo, 2 * e + 1)
                if n == 0:
                    pe.wait_ge(s_xl, c + 1)
                if not (isinstance(c, int) and c == 0 and n < AHEAD):
                    pe.wait_ge(s_gelu, NT_C * c + n - AHEAD + 1)
                products = [(w, x, k) for k in range(KD) for w, x in ((w1h, xTh), (w1h, xTl), (w1l, xTh))]
                for j, (w, x, k) in enumerate(products):
                    last = nc.tensor.matmul(psH[n % AHEAD][:, :], w[:, e, k, m * P:(m + 1) * P], x[slot][:, k, :],
                                            start=(j == 0), stop=(j == len(products) - 1))
                last.then_inc(s_h, 1)

            def second(c, n):
                e, m = n // M, n % M
                pe.wait_ge(s_hl, NT_C * c + n + 1)
                if m == 0:
                    pe.wait_ge(s_wlo, 2 * e + 2)
                k = n % RING
                for t in range(TILES):
                    for j, (h, w) in enumerate(((hidh, w2h), (hidh, w2l), (hidl, w2h))):
                        last = nc.tensor.matmul(psY[e % 2][:, t, :], h[k][:, t * P:(t + 1) * P], w[:, e, m, :],
                                                start=(m == 0 and j == 0 and t % 2 == 0),
                                                stop=(m == M - 1 and j == 2), skip_group_check=True)
                if m == M - 1:
                    last.then_inc(s_y, 1)

            def body(i, slot, last):
                c = 2 * i + slot
                for n in range(NT_C):
                    if n + AHEAD < NT_C:
                        hidden(c, slot, n + AHEAD)
                    elif not last:
                        hidden(c + 1, 1 - slot, n + AHEAD - NT_C)
                    second(c, n)
                    if not last:
                        prepare(n, i + slot, 1 - slot)

            pe.wait_ge(s_id, 2)
            pe.wait_ge(s_row, 48)
            nc.tensor.transpose(psM[:, 0:ROWS], rows[:, :], ident[0:ROWS, 0:ROWS]).then_inc(s_colps, 1)
            pe.wait_ge(s_cols, 1)
            for n in range(NT_C):
                if n == 19:
                    pe.wait_ge(s_small, 80)
                if n == 27:
                    pe.wait_ge(s_b2r, 2)
                prepare(n, 0, 0)
                if n == 19:
                    for first in range(AHEAD):
                        hidden(0, 0, first)
            loop(pe, body)


def layer(nc, x, adj, gnn_w, gnn_a, gamma, beta, wr, br, w1, b1, w2, b2, out, only_gnn=False):
    N, D = x.shape
    H, _, O = gnn_w.shape
    NT = N // P
    xt_dram = nc.dram_tensor("xt_scratch", [N, H * O], F32, kind="Internal").ap()
    s_dram = nc.dram_tensor("src_scratch", [H, N], F32, kind="Internal").ap()
    x1_dram = out if only_gnn else nc.dram_tensor("x1_scratch", [N, D], F32, kind="Internal").ap()
    with ExitStack() as graph:
        def sb(name, shape, dt=F32):
            return graph.enter_context(nc.sbuf_tensor(name, shape, dt))

        V = sb("V", [P, NT, 4, H, O + 1], F16)
        keep = {name: sb(name, [P, NT, H]) for name in ("cE", "cF", "dsharp")}
        keep["ndst"] = sb("ndst", [P, NT])
        with ExitStack() as rows:
            for name in ("E", "F"):
                keep[name] = rows.enter_context(nc.sbuf_tensor(name, [P, NT, H], F32))
            project(nc, x, gnn_w, gnn_a, xt_dram, s_dram, keep)
            split_rows(nc, xt_dram, V, keep, N, H, O)
        attend(nc, x, adj, s_dram, x1_dram, V, keep, H, O)
    if not only_gnn:
        mixture(nc, x1_dram, gamma, beta, wr, br, w1, b1, w2, b2, out)


_INS = ["x", "adj", "L0_gnn_W", "L0_gnn_a", "L0_ffn_gamma", "L0_ffn_beta", "L0_ffn_Wr", "L0_ffn_br",
        "L0_ffn_W1", "L0_ffn_b1", "L0_ffn_W2", "L0_ffn_b2"]


def kernel(**inputs):
    import numpy as _np
    import concourse.bacc as _bacc
    from concourse import mybir as _mybir
    from concourse.bass_utils import run_bass_kernel_spmd as _run

    nc = _bacc.Bacc("TRN2", target_bir_lowering=False, num_devices=1)
    arrays, args = {}, []
    for name in _INS:
        a = _np.ascontiguousarray(inputs[name])
        arrays[f"in_{name}"] = a
        args.append(nc.dram_tensor(f"in_{name}", a.shape, _mybir.dt.from_np(a.dtype), kind="ExternalInput").ap())
    out = nc.dram_tensor("out", inputs["x"].shape, _mybir.dt.float32, kind="ExternalOutput").ap()
    layer(nc, *args, out)
    r = _run(nc, [arrays], core_ids=[0])
    return r.results[0]["out"]
```
